# Optimizing a Trainium2 kernel written in Bass

```python
import numpy as np
import jax
import jax.numpy as jnp

def _softmax(x, axis=-1):
    return jax.nn.softmax(x, axis=axis)

def _gelu(x):
    return jax.nn.gelu(x, approximate=True)

def _silu(x):
    return jax.nn.silu(x)

def _sigmoid(x):
    return jax.nn.sigmoid(x)

def _layernorm(x, axis=-1, eps=1e-05):
    m = jnp.mean(x, axis=axis, keepdims=True)
    v = jnp.var(x, axis=axis, keepdims=True)
    return (x - m) / jnp.sqrt(v + eps)

def _scatter_add(tgt, idx, src, axis=0):
    return tgt.at[idx].add(src)

def _segment_sum(src, seg, n):
    return jax.ops.segment_sum(src, seg, n)
kernel_name = 'mk_cond_seq_d2_seqx_r4_5a461b'

def setup_inputs(seed: int=0):
    np.random.seed(seed)
    _w = jnp.asarray

    def _rec_inputs():
        import jax
        import jax.numpy as jnp
        _rk = jax.random.key(seed)
        x = -0.0002928 + 1 * jax.random.normal(jax.random.fold_in(_rk, 1), (2, 1024, 256), jnp.float32)
        _lenS = 1024 - jax.random.randint(jax.random.fold_in(_rk, 7), (2,), 0, max(1, 1024 // 4) + 1, jnp.int32)
        _lenS2 = 1024 - jax.random.randint(jax.random.fold_in(_rk, 8), (2,), 0, max(1, 1024 // 4) + 1, jnp.int32)
        itok_B_0_7 = jax.random.randint(jax.random.fold_in(_rk, 11), (2,), 0, 8, jnp.int32)
        condB_safetyscore = -0.927215 + 0.920279 * jax.random.normal(jax.random.fold_in(_rk, 12), (2,), jnp.float32)
        return (x, itok_B_0_7, condB_safetyscore)
    x, itok_B_0_7, condB_safetyscore = _rec_inputs()

    def _L0_cond_setup():
        import jax, jax.numpy as jnp
        import numpy as np
        E, H, I = (8, 256, 1024)
        B, S = (4, 256)
        LN_EPS = 1e-12
        key = jax.random.key(seed)
        ks = jax.random.split(key, 8)
        x = jax.random.normal(ks[0], (B, S, H), dtype=jnp.float32)
        expert_idx = jax.random.randint(ks[1], (B,), 0, E, dtype=jnp.int64)
        Wi = jax.random.normal(ks[2], (E, H, I), dtype=jnp.float32) * 0.02
        bi = jnp.zeros((E, I), dtype=jnp.float32)
        Wo = jax.random.normal(ks[3], (E, I, H), dtype=jnp.float32) * 0.02
        bo = jnp.zeros((E, H), dtype=jnp.float32)
        gamma = jnp.ones((E, H), dtype=jnp.float32)
        beta = jnp.zeros((E, H), dtype=jnp.float32)
        return {'input_tensor': x, 'expert_idx': expert_idx, 'Wi': Wi, 'bi': bi, 'Wo': Wo, 'bo': bo, 'gamma': gamma, 'beta': beta}
    _L0_cond_all = _L0_cond_setup()
    _L0_cond_in = {k: v for k, v in _L0_cond_all.items() if k in ('Wi', 'bi', 'Wo', 'bo', 'gamma', 'beta')}
    del _L0_cond_all

    def _L1_cond_setup():
        import jax, jax.numpy as jnp
        import numpy as np
        TEMPERATURE = 1.0
        ACT_THRESHOLD = 0.1
        MAX_ACT = 1.0
        SAFETY_KNOB = 1.0
        EPS = 1e-08

        def gram_schmidt(X):
            r = X.shape[1]
            Q = X
            for i in range(r):
                q = Q[:, i]
                q = q / (jnp.linalg.norm(q) + EPS)
                Q = Q.at[:, i].set(q)
                coeffs = q @ Q[:, i + 1:]
                Q = Q.at[:, i + 1:].add(-jnp.outer(q, coeffs))
            return Q
        key = jax.random.key(seed)
        ks = jax.random.split(key, 8)
        B, S, D, R = (8, 1024, 256, 32)
        init_std = 0.02
        return {'hidden_states': jax.random.normal(ks[0], (B, S, D), jnp.float32), 'safety_score': jax.random.normal(ks[1], (B,), jnp.float32), 'U': jax.random.normal(ks[2], (D, R), jnp.float32) * init_std, 'V': jax.random.normal(ks[3], (D, R), jnp.float32) * init_std, 'safety_bias': jnp.zeros((D,), jnp.float32), 'gate_w1': jax.random.normal(ks[4], (D // 4, D), jnp.float32) * (1.0 / np.sqrt(D)), 'gate_b1': jnp.zeros((D // 4,), jnp.float32), 'gate_w2': jax.random.normal(ks[5], (1, D // 4), jnp.float32) * (1.0 / np.sqrt(D // 4)), 'gate_b2': jnp.zeros((1,), jnp.float32), 'resp_w': jax.random.normal(ks[6], (D, R), jnp.float32) * (1.0 / np.sqrt(R)), 'resp_b': jnp.zeros((D,), jnp.float32)}
    _L1_cond_all = _L1_cond_setup()
    _L1_cond_in = {k: v for k, v in _L1_cond_all.items() if k in ('U', 'V', 'safety_bias', 'gate_w1', 'gate_b1', 'gate_w2', 'gate_b2', 'resp_w', 'resp_b')}
    del _L1_cond_all
    return {'x': x, 'itok_B_0_7': itok_B_0_7, 'condB_safetyscore': condB_safetyscore, 'L0_cond_Wi': _L0_cond_in['Wi'], 'L0_cond_bi': _L0_cond_in['bi'], 'L0_cond_Wo': _L0_cond_in['Wo'], 'L0_cond_bo': _L0_cond_in['bo'], 'L0_cond_gamma': _L0_cond_in['gamma'], 'L0_cond_beta': _L0_cond_in['beta'], 'L1_cond_U': _L1_cond_in['U'], 'L1_cond_V': _L1_cond_in['V'], 'L1_cond_safety_bias': _L1_cond_in['safety_bias'], 'L1_cond_gate_w1': _L1_cond_in['gate_w1'], 'L1_cond_gate_b1': _L1_cond_in['gate_b1'], 'L1_cond_gate_w2': _L1_cond_in['gate_w2'], 'L1_cond_gate_b2': _L1_cond_in['gate_b2'], 'L1_cond_resp_w': _L1_cond_in['resp_w'], 'L1_cond_resp_b': _L1_cond_in['resp_b']}

def reference(x, itok_B_0_7, condB_safetyscore, L0_cond_Wi, L0_cond_bi, L0_cond_Wo, L0_cond_bo, L0_cond_gamma, L0_cond_beta, L1_cond_U, L1_cond_V, L1_cond_safety_bias, L1_cond_gate_w1, L1_cond_gate_b1, L1_cond_gate_w2, L1_cond_gate_b2, L1_cond_resp_w, L1_cond_resp_b):
    import jax
    import jax.numpy as jnp

    def _L0_cond_ref(input_tensor, expert_idx, Wi, bi, Wo, bo, gamma, beta):
        import jax, jax.numpy as jnp
        import numpy as np
        E, H, I = (8, 256, 1024)
        B, S = (4, 256)
        LN_EPS = 1e-12
        Wi_b = Wi[expert_idx]
        bi_b = bi[expert_idx]
        Wo_b = Wo[expert_idx]
        bo_b = bo[expert_idx]
        g_b = gamma[expert_idx]
        be_b = beta[expert_idx]
        h = jax.nn.gelu(jnp.einsum('bsh,bhi->bsi', input_tensor, Wi_b) + bi_b[:, None, :], approximate=False)
        o = jnp.einsum('bsi,bih->bsh', h, Wo_b) + bo_b[:, None, :]
        r = o + input_tensor
        mu = jnp.mean(r, axis=-1, keepdims=True)
        var = jnp.mean(jnp.square(r - mu), axis=-1, keepdims=True)
        y = (r - mu) * jax.lax.rsqrt(var + LN_EPS)
        return y * g_b[:, None, :] + be_b[:, None, :]

    def _L1_cond_ref(hidden_states, safety_score, U, V, safety_bias, gate_w1, gate_b1, gate_w2, gate_b2, resp_w, resp_b):
        import jax, jax.numpy as jnp
        import numpy as np
        TEMPERATURE = 1.0
        ACT_THRESHOLD = 0.1
        MAX_ACT = 1.0
        SAFETY_KNOB = 1.0
        EPS = 1e-08

        def gram_schmidt(X):
            r = X.shape[1]
            Q = X
            for i in range(r):
                q = Q[:, i]
                q = q / (jnp.linalg.norm(q) + EPS)
                Q = Q.at[:, i].set(q)
                coeffs = q @ Q[:, i + 1:]
                Q = Q.at[:, i + 1:].add(-jnp.outer(q, coeffs))
            return Q
        R = resp_w.shape[1]
        U_o = gram_schmidt(U)
        V_o = gram_schmidt(V)
        basis = U_o @ V_o.T
        pooled = hidden_states.mean(axis=1)
        h1 = jax.nn.relu(pooled @ gate_w1.T + gate_b1)
        base_act = jax.nn.sigmoid(h1 @ gate_w2.T + gate_b2)
        mod = jax.nn.sigmoid(safety_score[:, None] / TEMPERATURE)
        knob = jnp.clip(jnp.asarray(SAFETY_KNOB, hidden_states.dtype), ACT_THRESHOLD, MAX_ACT)
        strength = (base_act * mod * knob)[:, None, :]
        proj = hidden_states @ basis
        feats = proj @ basis.T[:, :R]
        response = feats @ resp_w.T + resp_b + safety_bias
        return hidden_states + strength * response
    x = _L0_cond_ref(x, itok_B_0_7, L0_cond_Wi, L0_cond_bi, L0_cond_Wo, L0_cond_bo, L0_cond_gamma, L0_cond_beta)
    x = _L1_cond_ref(x, condB_safetyscore, L1_cond_U, L1_cond_V, L1_cond_safety_bias, L1_cond_gate_w1, L1_cond_gate_b1, L1_cond_gate_w2, L1_cond_gate_b2, L1_cond_resp_w, L1_cond_resp_b)
    return x

_drawn_inputs = setup_inputs


def setup_inputs(seed=0):
    import zlib

    import numpy as np

    out = dict(_drawn_inputs(seed))
    spreads = {'L0_cond_bi': (0.0, 0.1),
     'L0_cond_bo': (0.0, 0.1),
     'L0_cond_gamma': (1.0, 0.2),
     'L0_cond_beta': (0.0, 0.1),
     'L1_cond_safety_bias': (0.0, 2.0),
     'L1_cond_gate_b1': (0.0, 2.0),
     'L1_cond_resp_b': (0.0, 2.0)}
    factors = {'condB_safetyscore': 38.848,
     'L1_cond_V': 64.0,
     'L1_cond_gate_w1': 64.0,
     'L1_cond_gate_w2': 64.0,
     'L1_cond_U': 8.0,
     'L1_cond_resp_w': 8.0}
    for name, (base, spread) in spreads.items():
        noise = np.random.default_rng([zlib.crc32(name.encode()), seed]).standard_normal(out[name].shape)
        drawn = base * np.exp(spread * noise) if base else spread * noise
        out[name] = jnp.asarray(drawn.astype(out[name].dtype))
    for name, factor in factors.items():
        out[name] = (out[name] * factor).astype(out[name].dtype)
    return out
```

```python
from contextlib import ExitStack

import concourse.bass as bass
from concourse import mybir

P = 128
F32 = mybir.dt.float32
F32R = mybir.dt.float32r
I32 = mybir.dt.int32
ALU = mybir.AluOpType
ACT = mybir.ActivationFunctionType
AX_X = mybir.AxisListType.X

B, S, H = 2, 1024, 256
E, F = 8, 1024
R = 32
GH = 64
BT = 512
NB = B * S // BT
BPS = NB // B
TB = BT // P
TPS = S // P
NT = B * TPS
KH = H // P
NI = F // P
WC = 4
UPB = 3
LN_EPS = 1e-12
GS_EPS = 1e-8


def cond_seq_kernel(nc, x, itok, score, Wi, bi, Wo, bo, gamma, beta, U, V, safety_bias,
                    gate_w1, gate_b1, gate_w2, gate_b2, resp_w, resp_b, out):
    x_v = x.rearrange("b (n p) h -> p (b n) h", p=P)
    out_v = out.rearrange("b (n p) h -> p (b n) h", p=P)
    Wi_rows = Wi.rearrange("e h i -> (e h) i")
    Wo_rows = Wo.rearrange("e i h -> (e i) h")
    bi_rows = bi.rearrange("e (a p) -> (e a) p", p=P)

    with ExitStack() as ctx:
        def sb(name, shape, dt=F32):
            return ctx.enter_context(nc.sbuf_tensor(name, shape, dt))

        def bank(name):
            return ctx.enter_context(nc.psum_tensor(name, [P, 512], F32))

        def sem(name):
            return ctx.enter_context(nc.semaphore(name))

        xr = sb("xr", [P, NT, H])
        xT_hi = sb("xT_hi", [P, 2, KH, BT], F32R)
        xT_lo = sb("xT_lo", [P, 2, KH, BT], F32R)
        wi_raw = sb("wi_raw", [P, KH, F])
        wo_raw = sb("wo_raw", [P, NI, H])
        wi_hi = sb("wi_hi", [P, B, KH, F], F32R)
        wi_lo = sb("wi_lo", [P, B, KH, F], F32R)
        wo_hi = sb("wo_hi", [P, B, NI, H], F32R)
        wo_lo = sb("wo_lo", [P, B, NI, H], F32R)
        hf = sb("hf", [P, UPB, BT])
        h_hi = sb("h_hi", [P, NI, BT], F32R)
        h_lo = sb("h_lo", [P, NI, BT], F32R)
        hsT_hi = sb("hsT_hi", [P, 2, KH, BT], F32R)
        hsT_lo = sb("hsT_lo", [P, 2, KH, BT], F32R)
        hs_sum = sb("hs_sum", [P, NB, KH])
        rows3 = sb("rows3", [1, B, 3, H])
        bc3 = sb("bc3", [P, B, 3, H])
        bi_sb = sb("bi_sb", [B * NI, P])
        biT = sb("biT", [P, B * NI])
        bn6 = sb("bn6", [P, NT, 6])
        mv = sb("mv", [P, NT, 2])
        ve = sb("ve", [P, NT])
        rstd = sb("rstd", [P, NT])
        idx = sb("idx", [1, B], I32)
        ident = sb("ident", [P, P])
        below = sb("below", [P, P])
        half_neg = sb("half_neg", [P, 1])
        half_pos = sb("half_pos", [P, 1])
        neg_two = sb("neg_two", [P, 1])
        UV = sb("UV", [P, 2, KH, R])
        rw = sb("rw", [P, KH, R])
        UT = sb("UT", [R, H])
        rwT = sb("rwT", [R, H])
        mask = sb("mask", [2 * R, R])
        eye2 = sb("eye2", [2 * R, R])
        gram = sb("gram", [2 * R, R])
        gs = sb("gs", [2 * R, 2 * R])
        gs_row = sb("gs_row", [2 * R, 2, 2 * R])
        gs_n = sb("gs_n", [2 * R, R])
        gs_ne = sb("gs_ne", [2 * R, R])
        gs_f = sb("gs_f", [2 * R, R])
        gs_c = sb("gs_c", [2 * R, R])
        gs_d = sb("gs_d", [2 * R, R])
        gs_dn = sb("gs_dn", [2 * R, 1])
        gs_rn = sb("gs_rn", [2 * R, 1])
        Ln = sb("Ln", [2 * R, R])
        LnT = sb("LnT", [2 * R, R])
        gw_sb = sb("gw_sb", [2 * R, R])
        uo_top = sb("uo_top", [R, R])
        urep_hi = sb("urep_hi", [P, KH, 3, R], F32R)
        urep_lo = sb("urep_lo", [P, KH, 3, R], F32R)
        vtv = sb("vtv", [R, 3, R])
        ur = sb("ur", [R, H])
        g_hi = sb("g_hi", [P, H], F32R)
        resp_rhs = sb("resp_rhs", [P, H], F32R)
        bias_raw = sb("bias_raw", [P, H])
        row_w = sb("row_w", [P, 1])
        row_m = sb("row_m", [P, 1])
        row_t = sb("row_t", [P, 2])
        proj = sb("proj", [P, 2, BT], F32R)
        w1_sb = sb("w1_sb", [GH, H])
        w1T = sb("w1T", [P, KH, GH])
        b1c = sb("b1c", [GH, 1])
        w2c = sb("w2c", [GH, 1])
        w2rep = sb("w2rep", [GH, P])
        b2c = sb("b2c", [P, 1])
        b2h = sb("b2h", [P, 1])
        sc_sb = sb("sc_sb", [P, B])
        mod_t = sb("mod_t", [P, B])
        mod_s = sb("mod_s", [P, B])
        h1 = sb("h1", [GH, B])
        act_t = sb("act_t", [P, B])
        act_s = sb("act_s", [P, B])
        strength = sb("strength", [P, B])

        up = [bank(f"up{i}") for i in range(UPB)]
        dn = [bank(f"dn{i}") for i in range(2)]
        tp = [bank(f"tp{i}") for i in range(2)]
        misc = bank("misc")

        idx_in = sem("idx_in")
        x_in = [sem(f"x_in{i}") for i in range(NB)]
        wi_in = [sem(f"wi_in{i}") for i in range(WC + 1)]
        wo_in = [sem(f"wo_in{i}") for i in range(B)]
        bi_in = sem("bi_in")
        rows_in = [sem(f"rows_in{i}") for i in range(B)]
        uvr_in = sem("uvr_in")
        gate_in = sem("gate_in")
        w1_in = sem("w1_in")
        bias_in = sem("bias_in")
        out_done = sem("out_done")
        consts = sem("consts")
        setup_pe = sem("setup_pe")
        setup_act = sem("setup_act")
        setup_dve = sem("setup_dve")
        tp_done = sem("tp_done")
        tp_hi = sem("tp_hi")
        tp_lo = sem("tp_lo")
        wa_hi = sem("wa_hi")
        wd_lo = sem("wd_lo")
        wd_hi = sem("wd_hi")
        wp_lo = sem("wp_lo")
        up_done = sem("up_done")
        gelu_done = sem("gelu_done")
        hlo_done = sem("hlo_done")
        down_done = sem("down_done")
        r_done = sem("r_done")
        bc_done = sem("bc_done")
        xb_done = sem("xb_done")
        stat_done = sem("stat_done")
        rstd_done = sem("rstd_done")
        hs_done = sem("hs_done")
        row_done = sem("row_done")
        f_done = sem("f_done")
        gsu_done = sem("gsu_done")
        alg_pe = sem("alg_pe")
        alg_dve = sem("alg_dve")
        pj_done = sem("pj_done")
        pj_hi = sem("pj_hi")
        pj_lo = sem("pj_lo")
        z_done = sem("z_done")
        g_act = sem("g_act")
        str_done = sem("str_done")
        fin_pe = sem("fin_pe")
        fin_dve = sem("fin_dve")
        dve_seq = sem("dve_seq")
        pool_seq = sem("pool_seq")

        block = ctx.enter_context(nc.Block())

        def x_event(blk):
            return blk

        def hs_event(blk):
            return NB + blk

        fin_b0_banks = tp
        fin_b1_banks = up

        @block.sync
        def _(sp):
            sp.dma_start(idx[:], itok.rearrange("(a n) -> a n", a=1)).then_inc(idx_in, 16)
            sp.dma_start(xr[:, 0:TB, :], x_v[:, 0:TB, :]).then_inc(x_in[0], 16)
            sp.wait_ge(idx_in, 16)
            e = [sp.value_load(idx[0:1, b:b + 1], min_val=0, max_val=E - 1) for b in range(B)]

            def wi_of(b):
                return Wi_rows[bass.ds(e[b] * H, H), :].rearrange("(k p) i -> p k i", p=P)

            def wo_of(b):
                return Wo_rows[bass.ds(e[b] * F, F), :].rearrange("(k p) h -> p k h", p=P)

            def rows_of(b):
                for j, src in enumerate((bo, gamma, beta)):
                    sp.dma_start(rows3[0:1, b, j, :], src[bass.ds(e[b], 1), :]).then_inc(rows_in[b], 16)

            for c in range(WC):
                w = F // WC
                sp.dma_start(wi_raw[:, :, c * w:(c + 1) * w],
                             wi_of(0)[:, :, c * w:(c + 1) * w]).then_inc(wi_in[c], 16)
                if c == 0:
                    for b in range(B):
                        sp.dma_start(bi_sb[b * NI:(b + 1) * NI, :],
                                     bi_rows[bass.ds(e[b] * NI, NI), :]).then_inc(bi_in, 16)
            sp.dma_start(wo_raw[:], wo_of(0)).then_inc(wo_in[0], 16)
            rows_of(0)
            sp.dma_start(xr[:, TB:2 * TB, :], x_v[:, TB:2 * TB, :]).then_inc(x_in[1], 16)
            rows_of(1)
            sp.wait_ge(wa_hi, WC)
            sp.wait_ge(wd_lo, WC)
            sp.dma_start(wi_raw[:], wi_of(1)).then_inc(wi_in[WC], 16)
            for i in range(2, NB):
                sp.dma_start(xr[:, i * TB:(i + 1) * TB, :],
                             x_v[:, i * TB:(i + 1) * TB, :]).then_inc(x_in[i], 16)
            sp.wait_ge(wd_hi, WC)
            sp.wait_ge(wp_lo, WC)
            sp.dma_start(wo_raw[:], wo_of(1)).then_inc(wo_in[1], 16)
            n = 0
            for d in range(0, TPS, 2):
                sp.wait_ge(fin_dve, d + 2)
                sp.dma_start(out_v[:, d:d + 2, :], xr[:, d:d + 2, :]).then_inc(out_done, 16)
                n += 16
            for d in range(TPS, NT):
                sp.wait_ge(fin_dve, d + 1)
                sp.dma_start(out_v[:, d, :], xr[:, d, :]).then_inc(out_done, 16)
                n += 16
            sp.wait_ge(out_done, n)

        @block.gpsimd
        def _(pool):
            g = nc.gpsimd
            count = {}

            def finish(ins, done=pool_seq):
                count[done.name] = count.get(done.name, 0) + 1
                ins.then_inc(done, 1)
                pool.wait_ge(done, count[done.name])

            finish(g.memset(ident[:], 0.0))
            finish(g.memset(below[:], 1.0))
            finish(g.affine_select(out=ident[:], in_=ident[:], compare_op=ALU.not_equal, fill=1.0, base=0,
                                   pattern=[[-1, P]], channel_multiplier=1), consts)
            finish(g.affine_select(out=below[:], in_=below[:], compare_op=ALU.is_gt, fill=0.0, base=0,
                                   pattern=[[-1, P]], channel_multiplier=1), consts)
            finish(g.memset(half_pos[:], 0.5))
            finish(g.memset(half_neg[:], -0.5))
            finish(g.memset(neg_two[:], -2.0))
            finish(g.memset(bias_raw[:], 0.0))
            for j, src in enumerate((resp_b, safety_bias, resp_b, safety_bias)):
                pool.dma_start(bias_raw[96 + j:97 + j, :],
                               src.rearrange("(a n) -> a n", a=1)).then_inc(bias_in, 16)

            def gs_factor(i):
                pool.wait_ge(row_done, i + 1)
                d = gs_row[:, i % 2, i:i + 1]
                finish(g.tensor_tensor(gs_n[:, i:i + 1], d, half_pos[0:2 * R, :], ALU.pow))
                finish(g.tensor_scalar(gs_ne[:, i:i + 1], gs_n[:, i:i + 1], GS_EPS, None, ALU.add))
                finish(g.tensor_tensor(gs_f[:, i:i + 1], gs_ne[:, i:i + 1], neg_two[0:2 * R, :],
                                       ALU.pow), f_done)

            def weight_lo(c):
                pool.wait_ge(wd_hi, c + 1)
                m, j = divmod(c, WC)
                if m == 1:
                    w = F // WC
                    cut = slice(j * w, (j + 1) * w)
                    o, raw, hi = wi_lo[:, 1, :, cut], wi_raw[:, :, cut], wi_hi[:, 1, :, cut]
                else:
                    w = NI // WC
                    cut = slice(j * w, (j + 1) * w)
                    o, raw, hi = wo_lo[:, m // 2, cut, :], wo_raw[:, cut, :], wo_hi[:, m // 2, cut, :]
                finish(g.tensor_tensor(o, raw, hi.bitcast(F32), ALU.subtract), wp_lo)

            def spread_rows(b):
                pool.wait_ge(rows_in[b], 48)
                finish(g.partition_broadcast(bc3[:, b, :, :].rearrange("p j h -> p (j h)"),
                                             rows3[0:1, b, :, :].rearrange("p j h -> p (j h)")), bc_done)

            def add_bo(d):
                if d % TB == 0:
                    pool.wait_ge(tp_done, 2 * (x_event(d // TB) + 1))
                finish(g.tensor_tensor(xr[:, d, :], xr[:, d, :], bc3[:, d // TPS, 0, :], ALU.add), xb_done)

            def inv_std(d):
                pool.wait_ge(stat_done, d + 1)
                finish(g.tensor_tensor(rstd[:, d:d + 1], ve[:, d:d + 1], half_neg[:], ALU.pow), rstd_done)

            for blk in range(NB):
                for it in range(NI):
                    if blk < 2:
                        gs_factor(2 * NI * blk + it)
                    if blk == 0:
                        if it < WC:
                            weight_lo(it)
                        else:
                            if it == WC:
                                spread_rows(0)
                            add_bo(it - WC)
                    elif blk in (1, 2) and it % 2 == 1:
                        weight_lo(WC * blk + it // 2)
                    if blk >= 1 and it % 2 == 0:
                        if blk == 2 and it == 0:
                            spread_rows(1)
                        add_bo(blk * TB + it // 2)
                for t in range(TB):
                    if blk < 2:
                        gs_factor(2 * NI * blk + NI + 2 * t)
                        gs_factor(2 * NI * blk + NI + 2 * t + 1)
                    inv_std(blk * TB + t)

        @block.scalar
        def _(act):
            act.dma_start(UV[:, 0, :, :], U.rearrange("(k p) r -> p k r", p=P)).then_inc(uvr_in, 16)
            act.dma_start(UV[:, 1, :, :], V.rearrange("(k p) r -> p k r", p=P)).then_inc(uvr_in, 16)
            act.dma_start(rw[:], resp_w.rearrange("(k p) r -> p k r", p=P)).then_inc(uvr_in, 16)
            act.dma_start(w1_sb[:], gate_w1).then_inc(w1_in, 16)
            act.dma_start(b1c[:], gate_b1.rearrange("(n a) -> n a", a=1)).then_inc(gate_in, 16)
            act.dma_start(w2c[:], gate_w2.rearrange("a n -> n a")).then_inc(gate_in, 16)
            act.dma_start(b2c[:], gate_b2.rearrange("(a n) -> a n", a=1).to_broadcast([P, 1])).then_inc(gate_in, 16)
            act.dma_start(sc_sb[:], score.rearrange("(a n) -> a n", a=1).to_broadcast([P, B])).then_inc(gate_in, 16)

            def tp_evac(ev, dst, sums=None):
                for k in range(KH):
                    act.wait_ge(tp_done, 2 * ev + k + 1)
                    nc.scalar.activation(dst[:, k, :], tp[k][:], ACT.Copy,
                                         **({} if sums is None else {"accum_out": sums[:, k:k + 1]}))\
                      .then_inc(tp_hi, 1)

            def gelu(u):
                blk, it = divmod(u, NI)
                b = blk // BPS
                act.wait_ge(up_done, u + 1)
                if u >= UPB:
                    act.wait_ge(hlo_done, u - UPB + 1)
                bias = biT[:, b * NI + it:b * NI + it + 1]
                nc.scalar.activation(hf[:, u % UPB, :], up[u % UPB][:], ACT.Gelu, bias=bias)
                nc.scalar.activation(h_hi[:, it, :], up[u % UPB][:], ACT.Gelu, bias=bias)\
                  .then_inc(gelu_done, 1)

            def proj_hi(blk):
                act.wait_ge(pj_done, blk + 1)
                nc.scalar.activation(proj[0:96, blk % 2, :], misc[0:96, :], ACT.Copy).then_inc(pj_hi, 1)

            def gate(b):
                act.wait_ge(z_done, 2 * b + 1)
                nc.scalar.activation(h1[:, b:b + 1], misc[0:GH, 0:1], ACT.Relu, bias=b1c[:],
                                     scale=1.0 / S).then_inc(g_act, 1)
                act.wait_ge(z_done, 2 * b + 2)
                nc.scalar.activation(act_t[:, b:b + 1], misc[:, 4:5], ACT.Tanh, bias=b2h[:],
                                     scale=0.5).then_inc(g_act, 1)

            tp_evac(x_event(0), xT_hi[:, 0])
            act.wait_ge(gate_in, 64)
            nc.scalar.activation(mod_t[:], sc_sb[:], ACT.Tanh, scale=0.5).then_inc(setup_act, 1)
            act.wait_ge(setup_pe, 1)
            nc.scalar.activation(UT[:], dn[1][0:R, 0:H], ACT.Copy).then_inc(setup_act, 1)
            nc.scalar.activation(rwT[:], dn[1][0:R, H:2 * H], ACT.Copy).then_inc(setup_act, 1)
            for c in range(WC):
                w = F // WC
                act.wait_ge(wi_in[c], 16)
                nc.scalar.activation(wi_hi[:, 0, :, c * w:(c + 1) * w], wi_raw[:, :, c * w:(c + 1) * w],
                                     ACT.Copy).then_inc(wa_hi, 1)
                if c == 0:
                    act.wait_ge(setup_pe, 3)
                    nc.scalar.activation(w1T[:].rearrange("p k n -> p (k n)"),
                                         misc[:, 0:KH * GH], ACT.Copy).then_inc(setup_act, 1)
                    nc.scalar.activation(biT[:], misc[:, KH * GH:KH * GH + B * NI], ACT.Copy)\
                      .then_inc(setup_act, 1)
                    act.wait_ge(setup_act, 5)
            act.wait_ge(setup_dve, 3)
            for blk in range(NB):
                for it in range(NI):
                    gelu(blk * NI + it)
                if blk + 1 < NB:
                    tp_evac(x_event(blk + 1), xT_hi[:, (blk + 1) % 2])
                if blk == 2:
                    for s in range(2):
                        tp_evac(hs_event(s), hsT_hi[:, s], hs_sum[:, s, :])
                    proj_hi(0)
                    proj_hi(1)
                    gate(0)
                if blk == 3:
                    tp_evac(hs_event(2), hsT_hi[:, 0], hs_sum[:, 2, :])
                    proj_hi(2)
            tp_evac(hs_event(3), hsT_hi[:, 1], hs_sum[:, 3, :])
            gate(1)
            proj_hi(3)

        @block.vector
        def _(dve):
            v = nc.vector
            seq = [0]

            def link(ins):
                seq[0] += 1
                ins.then_inc(dve_seq, 1)
                dve.wait_ge(dve_seq, seq[0])

            def tp_rest(ev, hi, lo):
                for k in range(KH):
                    dve.wait_ge(tp_hi, 2 * ev + k + 1)
                    v.tensor_tensor(lo[:, k, :], tp[k][:], hi[:, k, :].bitcast(F32), ALU.subtract)\
                     .then_inc(tp_lo, 1)

            def weight_hi(c):
                m, j = divmod(c, WC)
                if m == 1:
                    w = F // WC
                    cut = slice(j * w, (j + 1) * w)
                    dve.wait_ge(wi_in[WC], 16)
                    o, raw = wi_hi[:, 1, :, cut], wi_raw[:, :, cut]
                else:
                    w = NI // WC
                    cut = slice(j * w, (j + 1) * w)
                    dve.wait_ge(wo_in[m // 2], 16)
                    o, raw = wo_hi[:, m // 2, cut, :], wo_raw[:, cut, :]
                v.tensor_copy(o, raw).then_inc(wd_hi, 1)

            def gs_spread(i):
                if i >= 1:
                    dve.wait_ge(gsu_done, i)
                v.stream_shuffle(gs_row[:, i % 2, :], gs[:], [i] * R).then_inc(row_done, 1)

            def gs_step(i):
                dve.wait_ge(f_done, i + 1)
                link(v.scalar_tensor_tensor(out=gs_c[:, i:i + 1], in0=gs[:, i:i + 1],
                                            scalar=gs_f[:, i:i + 1], in1=mask[:, i:i + 1],
                                            op0=ALU.mult, op1=ALU.mult))
                v.scalar_tensor_tensor(out=gs[:], in0=gs_row[:, i % 2, :], scalar=gs_c[:, i:i + 1],
                                       in1=gs[:], op0=ALU.mult, op1=ALU.subtract, reverse1=True)\
                 .then_inc(gsu_done, 1)
                if i + 1 < R:
                    gs_spread(i + 1)

            def h_low(u):
                dve.wait_ge(gelu_done, u + 1)
                v.tensor_tensor(h_lo[:, u % NI, :], hf[:, u % UPB, :],
                                h_hi[:, u % NI, :].bitcast(F32), ALU.subtract).then_inc(hlo_done, 1)

            def ln_stats(d):
                dve.wait_ge(xb_done, d + 1)
                dve.wait_ge(down_done, d + 1)
                v.tensor_tensor(xr[:, d, :], dn[d % 2][:, 0:H], xr[:, d, :], ALU.add).then_inc(r_done, 1)
                dve.wait_ge(r_done, d + 1)
                link(v.bn_stats(bn6[:, d, :], xr[:, d, :]))
                link(v.bn_aggr(mv[:, d, :], bn6[:, d, :]))
                v.tensor_scalar(ve[:, d:d + 1], mv[:, d, 1:2], LN_EPS, None, ALU.add).then_inc(stat_done, 1)

            def ln_apply(d):
                b = d // TPS
                link(v.scalar_tensor_tensor(out=xr[:, d, :], in0=xr[:, d, :], scalar=mv[:, d, 0:1],
                                            in1=bc3[:, b, 1, :], op0=ALU.subtract, op1=ALU.mult))
                dve.wait_ge(rstd_done, d + 1)
                v.scalar_tensor_tensor(out=xr[:, d, :], in0=xr[:, d, :], scalar=rstd[:, d:d + 1],
                                       in1=bc3[:, b, 2, :], op0=ALU.mult, op1=ALU.add)\
                 .then_inc(hs_done, 1)

            def proj_rest(blk):
                dve.wait_ge(pj_hi, blk + 1)
                v.tensor_tensor(proj[64:96, blk % 2, :], misc[64:96, :],
                                proj[64:96, blk % 2, :].bitcast(F32), ALU.subtract).then_inc(pj_lo, 1)

            def gate_strength(b):
                dve.wait_ge(g_act, 2 * b + 2)
                link(v.tensor_scalar(act_s[:, b:b + 1], act_t[:, b:b + 1], 0.5, 0.5, ALU.mult, ALU.add))
                v.tensor_tensor(strength[:, b:b + 1], act_s[:, b:b + 1], mod_s[:, b:b + 1], ALU.mult)\
                 .then_inc(str_done, 1)
                dve.wait_ge(str_done, b + 1)

            def final(d):
                b, j = divmod(d, TPS)
                banks = fin_b0_banks if b == 0 else fin_b1_banks
                dve.wait_ge(fin_pe, d + 1)
                v.scalar_tensor_tensor(out=xr[:, d, :], in0=banks[j % len(banks)][:, 0:H],
                                       scalar=strength[:, b:b + 1], in1=xr[:, d, :],
                                       op0=ALU.mult, op1=ALU.add).then_inc(fin_dve, 1)

            dve.wait_ge(consts, 2)
            for q in range(2):
                rows = slice(q * R, (q + 1) * R)
                v.tensor_copy(mask[rows, :], below[rows, rows])
                v.tensor_copy(eye2[rows, :], ident[rows, rows])
                v.tensor_copy(gs[rows, R:2 * R], ident[rows, rows])
            link(v.tensor_tensor(row_t[96:P, 0:1], ident[96:P, 96:97], ident[96:P, 97:98], ALU.add))
            link(v.tensor_tensor(row_m[96:P, :], ident[96:P, 98:99], ident[96:P, 99:100], ALU.add))
            link(v.tensor_tensor(row_w[96:P, :], row_t[96:P, 0:1], row_m[96:P, :], ALU.subtract))
            for s in range(2):
                v.tensor_copy(proj[96:P, s, :], row_w[96:P, :].to_broadcast([R, BT]))
            dve.wait_ge(setup_pe, 2)
            v.tensor_copy(gram[:], dn[0][0:2 * R, 0:R]).then_inc(setup_dve, 1)
            link(v.tensor_copy(gs[:, 0:R], dn[0][0:2 * R, 0:R]))
            gs_spread(0)
            tp_rest(x_event(0), xT_hi[:, 0], xT_lo[:, 0])
            dve.wait_ge(gate_in, 64)
            v.tensor_scalar(b2h[:], b2c[:], 0.5, None, ALU.mult).then_inc(setup_dve, 1)
            v.tensor_copy(w2rep[:], w2c[:].to_broadcast([GH, P])).then_inc(setup_dve, 1)
            dve.wait_ge(setup_act, 1)
            link(v.tensor_scalar(mod_s[:], mod_t[:], 0.5, 0.5, ALU.mult, ALU.add))
            dve.wait_ge(bias_in, 64)
            link(v.tensor_copy(g_hi[96:P, :], bias_raw[96:P, :]))
            v.scalar_tensor_tensor(out=resp_rhs[96:P, :], in0=bias_raw[96:P, :], scalar=row_m[96:P, :],
                                   in1=g_hi[96:P, :].bitcast(F32), op0=ALU.mult, op1=ALU.subtract,
                                   reverse1=True)
            for c in range(WC):
                w = F // WC
                dve.wait_ge(wa_hi, c + 1)
                v.tensor_tensor(wi_lo[:, 0, :, c * w:(c + 1) * w], wi_raw[:, :, c * w:(c + 1) * w],
                                wi_hi[:, 0, :, c * w:(c + 1) * w].bitcast(F32), ALU.subtract)\
                 .then_inc(wd_lo, 1)

            for blk in range(NB):
                for it in range(NI):
                    u = blk * NI + it
                    if blk < 2:
                        gs_step(2 * NI * blk + it)
                    if blk == 0 and it < WC:
                        weight_hi(it)
                    if blk in (1, 2) and it % 2 == 0:
                        weight_hi(WC * blk + it // 2)
                    h_low(u)
                    if blk >= 1 and it == 0:
                        ln_apply(blk * TB - 1)
                    if blk == 2 and it == 0:
                        link(v.tensor_tensor(gs_d[:], gs_ne[:], eye2[:], ALU.mult))
                        link(v.reduce_sum(gs_dn[:], gs_d[:], axis=AX_X))
                        link(v.reciprocal(gs_rn[:], gs_dn[:]))
                        link(v.tensor_scalar(Ln[:], gs[:, R:2 * R], gs_rn[:], None, ALU.mult))
                        v.transpose(LnT[:], Ln[:]).then_inc(alg_dve, 1)
                    if blk == 2 and it == 2:
                        dve.wait_ge(alg_pe, 1)
                        v.tensor_copy(gw_sb[R:2 * R, :], tp[0][R:2 * R, 0:R])
                        v.tensor_copy(uo_top[:], misc[0:R, 0:R]).then_inc(alg_dve, 1)
                        uo = misc[:, 0:KH * R].rearrange("p (k r) -> p k r", k=KH)
                        for k in range(KH):
                            last = v.tensor_copy(urep_hi[:, k, :, :],
                                                 uo[:, k, :].unsqueeze(1).to_broadcast([P, 3, R]))
                        link(last)
                        for k in range(KH):
                            last = v.tensor_tensor(urep_lo[:, k, :, :],
                                                   uo[:, k, :].unsqueeze(1).to_broadcast([P, 3, R]),
                                                   urep_hi[:, k, :, :].bitcast(F32), ALU.subtract)
                        last.then_inc(alg_dve, 1)
                    if blk == 2 and it == 4:
                        dve.wait_ge(alg_pe, 2)
                        v.tensor_copy(vtv[:], tp[0][0:R, 0:R].unsqueeze(1).to_broadcast([R, 3, R]))
                        v.tensor_copy(ur[:], misc[0:R, 0:H]).then_inc(alg_dve, 1)
                    if blk == 2 and it == 6:
                        dve.wait_ge(alg_pe, 3)
                        link(v.tensor_copy(g_hi[0:96, :], misc[0:96, 0:H]))
                        v.tensor_copy(resp_rhs[0:R, :], g_hi[0:R, :].bitcast(F32))
                        v.tensor_copy(resp_rhs[2 * R:3 * R, :], g_hi[2 * R:3 * R, :].bitcast(F32))
                        v.tensor_tensor(resp_rhs[R:2 * R, :], misc[R:2 * R, 0:H],
                                        g_hi[R:2 * R, :].bitcast(F32), ALU.subtract).then_inc(alg_dve, 1)
                    if blk == 3:
                        final(it)
                if blk + 1 < NB:
                    s = (blk + 1) % 2
                    tp_rest(x_event(blk + 1), xT_hi[:, s], xT_lo[:, s])
                for t in range(TB):
                    if blk < 2:
                        gs_step(2 * NI * blk + NI + 2 * t)
                    if blk == 2 and t < 2:
                        tp_rest(hs_event(t), hsT_hi[:, t], hsT_lo[:, t])
                    if blk == 2 and t >= 2:
                        proj_rest(t - 2)
                    if blk == 3 and t == 1:
                        tp_rest(hs_event(2), hsT_hi[:, 0], hsT_lo[:, 0])
                    if blk == 3 and t == 3:
                        proj_rest(2)
                    ln_stats(blk * TB + t)
                    if blk < 2:
                        gs_step(2 * NI * blk + NI + 2 * t + 1)
                    if t >= 1:
                        ln_apply(blk * TB + t - 1)
                if blk == 2:
                    gate_strength(0)
            ln_apply(NT - 1)
            tp_rest(hs_event(3), hsT_hi[:, 1], hsT_lo[:, 1])
            gate_strength(1)
            proj_rest(3)
            for j in range(TPS):
                final(TPS + j)

        @block.tensor
        def _(pe):
            def x_transposes(blk):
                ev = x_event(blk)
                pe.wait_ge(x_in[blk], 16)
                for k in range(KH):
                    if ev >= 1:
                        pe.wait_ge(tp_lo, 2 * (ev - 1) + k + 1)
                    for t in range(TB):
                        last = nc.tensor.transpose(tp[k][:, t * P:(t + 1) * P],
                                                   xr[:, blk * TB + t, k * P:(k + 1) * P], ident[:])
                    last.then_inc(tp_done, 1)

            def hs_transposes(blk):
                ev = hs_event(blk)
                pe.wait_ge(hs_done, (blk + 1) * TB)
                for k in range(KH):
                    pe.wait_ge(tp_lo, 2 * (ev - 1) + k + 1)
                    if blk == 2:
                        pe.wait_ge(fin_dve, TPS)
                    for t in range(TB):
                        last = nc.tensor.transpose(tp[k][:, t * P:(t + 1) * P],
                                                   xr[:, blk * TB + t, k * P:(k + 1) * P], ident[:])
                    last.then_inc(tp_done, 1)

            def up_unit(u):
                blk, it = divmod(u, NI)
                b, s = blk // BPS, blk % 2
                if u >= UPB:
                    pe.wait_ge(gelu_done, u - UPB + 1)
                if it == 0:
                    pe.wait_ge(tp_lo, 2 * (x_event(blk) + 1))
                if b == 0 and blk == 0:
                    pe.wait_ge(wd_lo, it * WC // NI + 1)
                elif blk == BPS:
                    pe.wait_ge(wp_lo, WC + it * WC // NI + 1)
                cut = slice(it * P, (it + 1) * P)
                parts = [(wi_hi, xT_hi), (wi_hi, xT_lo), (wi_lo, xT_hi)]
                for k in range(KH):
                    for n, (w, xs) in enumerate(parts):
                        last = nc.tensor.matmul(up[u % UPB][:], w[:, b, k, cut], xs[:, s, k, :],
                                                start=(k == 0 and n == 0),
                                                stop=(k == KH - 1 and n == len(parts) - 1))
                last.then_inc(up_done, 1)

            def down_tile(d):
                blk, t = divmod(d, TB)
                b = blk // BPS
                if d >= 2:
                    pe.wait_ge(r_done, d - 1)
                cut = slice(t * P, (t + 1) * P)
                parts = [(h_hi, wo_hi), (h_hi, wo_lo), (h_lo, wo_hi)]
                for k in range(NI):
                    if t == 0:
                        pe.wait_ge(hlo_done, blk * NI + k + 1)
                        if blk % BPS == 0:
                            pe.wait_ge(wp_lo, 2 * WC * b + k * WC // NI + 1)
                    for n, (h, w) in enumerate(parts):
                        last = nc.tensor.matmul(dn[d % 2][:, 0:H], h[:, k, cut], w[:, b, k, :],
                                                start=(k == 0 and n == 0),
                                                stop=(k == NI - 1 and n == len(parts) - 1))
                last.then_inc(down_done, 1)

            def project(blk):
                if blk == 0:
                    pe.wait_ge(alg_dve, 5)
                else:
                    pe.wait_ge(pj_lo, blk)
                if blk == 3:
                    pe.wait_ge(g_act, 4)
                if blk == 2:
                    pe.wait_ge(g_act, 2)
                pe.wait_ge(tp_lo, 2 * (hs_event(blk) + 1))
                parts = [(urep_hi, hsT_hi), (urep_lo, hsT_hi), (urep_hi, hsT_lo)]
                for k in range(KH):
                    for n, (w, hs) in enumerate(parts):
                        last = nc.tensor.matmul(misc[0:96, :], w[:, k, :, :].rearrange("p j r -> p (j r)"),
                                                hs[:, blk % 2, k, :], start=(k == 0 and n == 0),
                                                stop=(k == KH - 1 and n == len(parts) - 1))
                last.then_inc(pj_done, 1)

            def gate(b):
                pe.wait_ge(tp_hi, 2 * (hs_event(b * BPS + BPS - 1) + 1))
                n = 0
                for s in range(BPS):
                    for k in range(KH):
                        last = nc.tensor.matmul(misc[0:GH, 0:1], w1T[:, k, :],
                                                hs_sum[:, b * BPS + s, k:k + 1], start=(n == 0),
                                                stop=(n == BPS * KH - 1))
                        n += 1
                last.then_inc(z_done, 1)
                pe.wait_ge(g_act, 2 * b + 1)
                nc.tensor.matmul(misc[:, 4:5], w2rep[:], h1[:, b:b + 1], start=True, stop=True)\
                  .then_inc(z_done, 1)

            def response(d):
                b, j = divmod(d, TPS)
                banks = fin_b0_banks if b == 0 else fin_b1_banks
                blk, t = divmod(d, TB)
                pe.wait_ge(pj_lo, blk + 1)
                if j >= len(banks):
                    pe.wait_ge(fin_dve, d - len(banks) + 1)
                nc.tensor.matmul(banks[j % len(banks)][:, 0:H], proj[:, blk % 2, t * P:(t + 1) * P],
                                 resp_rhs[:], start=True, stop=True).then_inc(fin_pe, 1)

            pe.wait_ge(consts, 2)
            x_transposes(0)
            pe.wait_ge(uvr_in, 48)
            for k in range(KH):
                nc.tensor.transpose(dn[1][0:R, k * P:(k + 1) * P], UV[:, 0, k, :], ident[:])
            for k in range(KH):
                last = nc.tensor.transpose(dn[1][0:R, H + k * P:H + (k + 1) * P], rw[:, k, :], ident[:])
            last.then_inc(setup_pe, 1)
            for m in range(2):
                for k in range(KH):
                    last = nc.tensor.matmul(dn[0][m * R:(m + 1) * R, 0:R], UV[:, m, k, :], UV[:, m, k, :],
                                            start=(k == 0), stop=(k == KH - 1))
            last.then_inc(setup_pe, 1)
            pe.wait_ge(w1_in, 16)
            for k in range(KH):
                nc.tensor.transpose(misc[:, k * GH:(k + 1) * GH], w1_sb[:, k * P:(k + 1) * P],
                                    ident[0:GH, 0:GH])
            pe.wait_ge(bi_in, 32)
            nc.tensor.transpose(misc[:, KH * GH:KH * GH + B * NI], bi_sb[:],
                                ident[0:B * NI, 0:B * NI]).then_inc(setup_pe, 1)

            for blk in range(NB):
                for it in range(NI):
                    up_unit(blk * NI + it)
                    if blk == 2 and it == 1:
                        pe.wait_ge(alg_dve, 1)
                        pe.wait_ge(setup_act, 5)
                        nc.tensor.matmul(tp[0][R:2 * R, 0:R], gram[R:2 * R, :], LnT[R:2 * R, :],
                                         start=True, stop=True)
                        for k in range(KH):
                            last = nc.tensor.matmul(misc[:, k * R:(k + 1) * R], UT[:, k * P:(k + 1) * P],
                                                    LnT[0:R, :], start=True, stop=True)
                        last.then_inc(alg_pe, 1)
                    if blk == 2 and it == 3:
                        pe.wait_ge(alg_dve, 3)
                        nc.tensor.matmul(tp[0][0:R, 0:R], LnT[R:2 * R, :], gw_sb[R:2 * R, :],
                                         start=True, stop=True)
                        nc.tensor.matmul(misc[0:R, 0:H], uo_top[:], rwT[:], start=True, stop=True)\
                          .then_inc(alg_pe, 1)
                    if blk == 2 and it == 5:
                        pe.wait_ge(alg_dve, 4)
                        nc.tensor.matmul(misc[0:96, 0:H], vtv[:].rearrange("p j r -> p (j r)"), ur[:],
                                         start=True, stop=True).then_inc(alg_pe, 1)
                    if blk == 3:
                        if it == 0:
                            pe.wait_ge(tp_lo, 2 * (hs_event(1) + 1))
                        response(it)
                if blk + 1 < NB:
                    x_transposes(blk + 1)
                for t in range(TB):
                    down_tile(blk * TB + t)
                    if blk == 2 and t < 2:
                        hs_transposes(t)
                    if blk == 2 and t >= 2:
                        project(t - 2)
                    if blk == 3 and t == 0:
                        hs_transposes(2)
                    if blk == 3 and t == 2:
                        project(2)
                if blk == 2:
                    pe.wait_ge(pj_lo, 2)
                    gate(0)
            hs_transposes(3)
            pe.wait_ge(pj_lo, 3)
            gate(1)
            project(3)
            for j in range(TPS):
                response(TPS + j)


_INS = ["x", "itok_B_0_7", "condB_safetyscore", "L0_cond_Wi", "L0_cond_bi", "L0_cond_Wo", "L0_cond_bo",
        "L0_cond_gamma", "L0_cond_beta", "L1_cond_U", "L1_cond_V", "L1_cond_safety_bias",
        "L1_cond_gate_w1", "L1_cond_gate_b1", "L1_cond_gate_w2", "L1_cond_gate_b2", "L1_cond_resp_w",
        "L1_cond_resp_b"]


def kernel(**inputs):
    import numpy as _np
    import concourse.bacc as _bacc
    from concourse import mybir as _mybir
    from concourse.bass_utils import run_bass_kernel_spmd as _run

    nc = _bacc.Bacc("TRN2", target_bir_lowering=False, num_devices=1)
    arrays, args = {}, []
    for name in _INS:
        a = _np.ascontiguousarray(inputs[name])
        arrays[f"in_{name}"] = a
        args.append(nc.dram_tensor(f"in_{name}", a.shape, _mybir.dt.from_np(a.dtype), kind="ExternalInput").ap())
    out = nc.dram_tensor("out_0", (B, S, H), _mybir.dt.float32, kind="ExternalOutput").ap()
    cond_seq_kernel(nc, *args, out)
    r = _run(nc, [arrays], core_ids=[0])
    return r.results[0]["out_0"]
```

```python
from contextlib import ExitStack

import concourse.bass as bass
from concourse import mybir

P = 128
F32 = mybir.dt.float32
F32R = mybir.dt.float32r
I32 = mybir.dt.int32
ALU = mybir.AluOpType
ACT = mybir.ActivationFunctionType
AX_X = mybir.AxisListType.X

B, S, H = 2, 1024, 256
E, F = 8, 1024
R = 32
GH = 64
BT = 512
NB = B * S // BT
BPS = NB // B
TB = BT // P
TPS = S // P
NT = B * TPS
KH = H // P
NI = F // P
WC = 4
UPB = 3
LN_EPS = 1e-12
GS_EPS = 1e-8


def cond_seq_kernel(nc, x, itok, score, Wi, bi, Wo, bo, gamma, beta, U, V, safety_bias,
                    gate_w1, gate_b1, gate_w2, gate_b2, resp_w, resp_b, out):
    x_v = x.rearrange("b (n p) h -> p (b n) h", p=P)
    out_v = out.rearrange("b (n p) h -> p (b n) h", p=P)
    Wi_rows = Wi.rearrange("e h i -> (e h) i")
    Wo_rows = Wo.rearrange("e i h -> (e i) h")
    bi_rows = bi.rearrange("e (a p) -> (e a) p", p=P)

    with ExitStack() as ctx:
        def sb(name, shape, dt=F32):
            return ctx.enter_context(nc.sbuf_tensor(name, shape, dt))

        def bank(name):
            return ctx.enter_context(nc.psum_tensor(name, [P, 512], F32))

        def sem(name):
            return ctx.enter_context(nc.semaphore(name))

        xr = sb("xr", [P, NT, H])
        xT_hi = sb("xT_hi", [P, 2, KH, BT], F32R)
        xT_lo = sb("xT_lo", [P, 2, KH, BT], F32R)
        wi_raw = sb("wi_raw", [P, KH, F])
        wo_raw = sb("wo_raw", [P, NI, H])
        wi_hi = sb("wi_hi", [P, B, KH, F], F32R)
        wi_lo = sb("wi_lo", [P, B, KH, F], F32R)
        wo_hi = sb("wo_hi", [P, B, NI, H], F32R)
        wo_lo = sb("wo_lo", [P, B, NI, H], F32R)
        hf = sb("hf", [P, UPB, BT])
        h_hi = sb("h_hi", [P, NI, BT], F32R)
        h_lo = sb("h_lo", [P, NI, BT], F32R)
        hsT = sb("hsT", [P, NB, KH, BT])
        hs_sum = sb("hs_sum", [P, NB, KH])
        rows3 = sb("rows3", [1, B, 3, H])
        bc3 = sb("bc3", [P, B, 3, H])
        bi_sb = sb("bi_sb", [B * NI, P])
        biT = sb("biT", [P, B * NI])
        bn6 = sb("bn6", [P, NT, 6])
        mv = sb("mv", [P, NT, 2])
        ve = sb("ve", [P, NT])
        rstd = sb("rstd", [P, NT])
        idx = sb("idx", [1, B], I32)
        ident = sb("ident", [P, P])
        below = sb("below", [P, P])
        half_neg = sb("half_neg", [P, 1])
        half_pos = sb("half_pos", [P, 1])
        neg_two = sb("neg_two", [P, 1])
        UV = sb("UV", [P, 2, KH, R])
        rw = sb("rw", [P, KH, R])
        UT = sb("UT", [R, H])
        rwT = sb("rwT", [R, H])
        mask = sb("mask", [2 * R, R])
        eye2 = sb("eye2", [2 * R, R])
        gram = sb("gram", [2 * R, R])
        gs = sb("gs", [2 * R, 2 * R])
        gs_row = sb("gs_row", [2 * R, 2, 2 * R])
        gs_old = sb("gs_old", [2 * R, 2 * R])
        gs_k = sb("gs_k", [2 * R, R])
        gs_n = sb("gs_n", [2 * R, R])
        gs_ne = sb("gs_ne", [2 * R, R])
        gs_f = sb("gs_f", [2 * R, R])
        gs_c = sb("gs_c", [2 * R, R])
        gs_d = sb("gs_d", [2 * R, R])
        gs_dn = sb("gs_dn", [2 * R, 1])
        gs_rn = sb("gs_rn", [2 * R, 1])
        Ln = sb("Ln", [2 * R, R])
        LnT = sb("LnT", [2 * R, R])
        gw_sb = sb("gw_sb", [2 * R, R])
        uo_top = sb("uo_top", [R, R])
        urep = sb("urep", [P, KH, 3, R])
        vtv = sb("vtv", [R, 3, R])
        ur = sb("ur", [R, H])
        g_hi = sb("g_hi", [P, H], F32R)
        resp_rhs = sb("resp_rhs", [P, H], F32R)
        bias_raw = sb("bias_raw", [P, H])
        row_w = sb("row_w", [P, 1])
        row_m = sb("row_m", [P, 1])
        row_t = sb("row_t", [P, 2])
        proj = sb("proj", [P, NB, BT], F32R)
        w1_sb = sb("w1_sb", [GH, H])
        w1T = sb("w1T", [P, KH, GH])
        b1c = sb("b1c", [GH, 1])
        w2c = sb("w2c", [GH, 1])
        w2rep = sb("w2rep", [GH, P])
        b2c = sb("b2c", [P, 1])
        b2h = sb("b2h", [P, 1])
        sc_sb = sb("sc_sb", [P, B])
        mod_t = sb("mod_t", [P, B])
        mod_s = sb("mod_s", [P, B])
        h1 = sb("h1", [GH, B])
        act_t = sb("act_t", [P, B])
        act_s = sb("act_s", [P, B])
        strength = sb("strength", [P, B])

        up = [bank(f"up{i}") for i in range(UPB)]
        dn = [bank(f"dn{i}") for i in range(2)]
        tp = [bank(f"tp{i}") for i in range(2)]
        misc = bank("misc")

        idx_in = sem("idx_in")
        x_in = [sem(f"x_in{i}") for i in range(NB)]
        wi_in = [sem(f"wi_in{i}") for i in range(WC + 1)]
        wo_in = [sem(f"wo_in{i}") for i in range(B)]
        bi_in = sem("bi_in")
        rows_in = [sem(f"rows_in{i}") for i in range(B)]
        uv_in = sem("uv_in")
        rw_in = sem("rw_in")
        gate_in = sem("gate_in")
        bias_in = sem("bias_in")
        out_done = sem("out_done")
        consts = sem("consts")
        gram_pe = sem("gram_pe")
        setup_pe = sem("setup_pe")
        setup_act = sem("setup_act")
        gate_act = sem("gate_act")
        gate_dve = sem("gate_dve")
        tx_done = sem("tx_done")
        tx_hi = sem("tx_hi")
        tx_lo = sem("tx_lo")
        th_done = sem("th_done")
        th_out = sem("th_out")
        wi0_hi = sem("wi0_hi")
        wi0_lo = sem("wi0_lo")
        wo0_hi = sem("wo0_hi")
        wo0_lo_d = sem("wo0_lo_d")
        wo0_lo_p = sem("wo0_lo_p")
        w1_hi = sem("w1_hi")
        wi1_lo = sem("wi1_lo")
        wo1_lo = sem("wo1_lo")
        up_done = sem("up_done")
        gelu_done = sem("gelu_done")
        hlo_done = sem("hlo_done")
        down_done = sem("down_done")
        r_done = sem("r_done")
        bc_done = sem("bc_done")
        xb_done = sem("xb_done")
        bn_done = sem("bn_done")
        mv_done = sem("mv_done")
        stat_done = sem("stat_done")
        rstd_done = sem("rstd_done")
        y_done = sem("y_done")
        hs_done = sem("hs_done")
        old_done = sem("old_done")
        key_done = sem("key_done")
        row_done = sem("row_done")
        f_done = sem("f_done")
        gsu_done = sem("gsu_done")
        alg_pe = sem("alg_pe")
        alg_dve = sem("alg_dve")
        rhs_dve = sem("rhs_dve")
        pj_done = sem("pj_done")
        pj_hi = sem("pj_hi")
        pj_lo = sem("pj_lo")
        z_done = sem("z_done")
        g_act = sem("g_act")
        str_done = sem("str_done")
        fin_pe = sem("fin_pe")
        fin_dve = sem("fin_dve")
        dve_seq = sem("dve_seq")
        pool_seq = sem("pool_seq")

        block = ctx.enter_context(nc.Block())

        GS0 = 4
        WCUT = F // WC
        KCUT = NI // WC
        WO_D = 2
        resp_banks = [up[2], dn[0], dn[1]]

        def gs_slot(blk, it):
            return GS0 + blk * (NI // 2 + TB) + it // 2

        def wi_cut(t, b, c):
            return t[:, b, :, c * WCUT:(c + 1) * WCUT]

        def wo_cut(t, b, c):
            return t[:, b, c * KCUT:(c + 1) * KCUT, :]

        @block.sync
        def _(sp):
            sp.dma_start(idx[:], itok.rearrange("(a n) -> a n", a=1)).then_inc(idx_in, 16)
            sp.dma_start(xr[:, 0:TB, :], x_v[:, 0:TB, :]).then_inc(x_in[0], 16)
            sp.dma_start(UV[:, 0, :, :], U.rearrange("(k p) r -> p k r", p=P)).then_inc(uv_in, 16)
            sp.wait_ge(idx_in, 16)
            e = [sp.value_load(idx[0:1, b:b + 1], min_val=0, max_val=E - 1) for b in range(B)]

            def wi_of(b):
                return Wi_rows[bass.ds(e[b] * H, H), :].rearrange("(k p) i -> p k i", p=P)

            def wo_of(b):
                return Wo_rows[bass.ds(e[b] * F, F), :].rearrange("(k p) h -> p k h", p=P)

            def rows_of(b):
                for j, src in enumerate((bo, gamma, beta)):
                    sp.dma_start(rows3[0:1, b, j, :], src[bass.ds(e[b], 1), :]).then_inc(rows_in[b], 16)

            for c in range(WC):
                cut = slice(c * WCUT, (c + 1) * WCUT)
                sp.dma_start(wi_raw[:, :, cut], wi_of(0)[:, :, cut]).then_inc(wi_in[c], 16)
                if c == 0:
                    for b in range(B):
                        sp.dma_start(bi_sb[b * NI:(b + 1) * NI, :],
                                     bi_rows[bass.ds(e[b] * NI, NI), :]).then_inc(bi_in, 16)
            rows_of(0)
            sp.dma_start(wo_raw[:], wo_of(0)).then_inc(wo_in[0], 16)
            sp.dma_start(xr[:, TB:2 * TB, :], x_v[:, TB:2 * TB, :]).then_inc(x_in[1], 16)
            sp.dma_start(w1_sb[:], gate_w1).then_inc(gate_in, 16)
            sp.dma_start(b1c[:], gate_b1.rearrange("(n a) -> n a", a=1)).then_inc(gate_in, 16)
            sp.dma_start(w2c[:], gate_w2.rearrange("a n -> n a")).then_inc(gate_in, 16)
            sp.dma_start(b2c[:], gate_b2.rearrange("(a n) -> a n", a=1).to_broadcast([P, 1])).then_inc(gate_in, 16)
            sp.dma_start(sc_sb[:], score.rearrange("(a n) -> a n", a=1).to_broadcast([P, B])).then_inc(gate_in, 16)
            sp.dma_start(rw[:], resp_w.rearrange("(k p) r -> p k r", p=P)).then_inc(rw_in, 16)
            rows_of(1)
            sp.wait_ge(consts, 3)
            for j, src in enumerate((resp_b, safety_bias, resp_b, safety_bias)):
                sp.dma_start(bias_raw[96 + j:97 + j, :],
                             src.rearrange("(a n) -> a n", a=1)).then_inc(bias_in, 16)
            sp.wait_ge(wi0_hi, WC)
            sp.wait_ge(wi0_lo, WC)
            sp.dma_start(wi_raw[:], wi_of(1)).then_inc(wi_in[WC], 16)
            for i in range(2, NB):
                sp.dma_start(xr[:, i * TB:(i + 1) * TB, :],
                             x_v[:, i * TB:(i + 1) * TB, :]).then_inc(x_in[i], 16)
            sp.wait_ge(wo0_hi, WC)
            sp.wait_ge(wo0_lo_d, WO_D)
            sp.wait_ge(wo0_lo_p, WC - WO_D)
            sp.dma_start(wo_raw[:], wo_of(1)).then_inc(wo_in[1], 16)
            n = 0
            for d in range(0, TPS, 2):
                sp.wait_ge(fin_dve, d + 2)
                sp.dma_start(out_v[:, d:d + 2, :], xr[:, d:d + 2, :]).then_inc(out_done, 16)
                n += 16
            for d in range(TPS, NT):
                sp.wait_ge(fin_dve, d + 1)
                sp.dma_start(out_v[:, d, :], xr[:, d, :]).then_inc(out_done, 16)
                n += 16
            sp.wait_ge(out_done, n)

        @block.gpsimd
        def _(pool):
            g = nc.gpsimd
            count = {}

            def finish(ins, done=pool_seq):
                count[done.name] = count.get(done.name, 0) + 1
                ins.then_inc(done, 1)
                pool.wait_ge(done, count[done.name])

            finish(g.memset(ident[:], 0.0))
            finish(g.affine_select(out=ident[:], in_=ident[:], compare_op=ALU.not_equal, fill=1.0, base=0,
                                   pattern=[[-1, P]], channel_multiplier=1), consts)
            finish(g.memset(below[:], 1.0))
            finish(g.affine_select(out=below[:], in_=below[:], compare_op=ALU.is_gt, fill=0.0, base=0,
                                   pattern=[[-1, P]], channel_multiplier=1), consts)
            finish(g.memset(half_pos[:], 0.5))
            finish(g.memset(half_neg[:], -0.5))
            finish(g.memset(neg_two[:], -2.0))
            finish(g.memset(bias_raw[:], 0.0), consts)

            def gs_factor(i):
                pool.wait_ge(row_done, i + 1)
                d = gs_row[:, i % 2, i:i + 1]
                finish(g.tensor_tensor(gs_n[:, i:i + 1], d, half_pos[0:2 * R, :], ALU.pow))
                finish(g.tensor_scalar(gs_ne[:, i:i + 1], gs_n[:, i:i + 1], GS_EPS, None, ALU.add))
                finish(g.tensor_tensor(gs_f[:, i:i + 1], gs_ne[:, i:i + 1], neg_two[0:2 * R, :],
                                       ALU.pow), f_done)

            def wo_lo_part(b, c, hi_done, n, done):
                pool.wait_ge(hi_done, n)
                finish(g.tensor_tensor(wo_cut(wo_lo, b, c), wo_raw[:, c * KCUT:(c + 1) * KCUT, :],
                                       wo_cut(wo_hi, b, c).bitcast(F32), ALU.subtract), done)

            def spread_rows(b):
                pool.wait_ge(rows_in[b], 48)
                finish(g.partition_broadcast(bc3[:, b, :, :].rearrange("p j h -> p (j h)"),
                                             rows3[0:1, b, :, :].rearrange("p j h -> p (j h)")), bc_done)

            def add_bo(d):
                if d % TB == 0:
                    pool.wait_ge(tx_done, KH * (d // TB + 1))
                finish(g.tensor_tensor(xr[:, d, :], xr[:, d, :], bc3[:, d // TPS, 0, :], ALU.add), xb_done)

            def inv_std(d):
                pool.wait_ge(stat_done, d + 1)
                finish(g.tensor_tensor(rstd[:, d:d + 1], ve[:, d:d + 1], half_neg[:], ALU.pow), rstd_done)

            for i in range(GS0):
                gs_factor(i)
            spread_rows(0)
            gs_factor(GS0)
            add_bo(0)
            for blk in range(NB):
                for it in range(NI):
                    if it % 2 == 0:
                        if gs_slot(blk, it) + 1 < R:
                            gs_factor(gs_slot(blk, it) + 1)
                        if blk == 0:
                            if it // 2 < WC - WO_D:
                                c = it // 2
                                wo_lo_part(0, c, wo0_hi, c + 1, wo0_lo_p)
                            elif it == 4:
                                add_bo(1)
                                add_bo(2)
                            else:
                                add_bo(3)
                    if it % 2 == 1 and blk >= 1:
                        if blk == BPS and it == 1:
                            spread_rows(1)
                        add_bo(blk * TB + it // 2)
                        if blk == BPS and it // 2 >= 2:
                            c = it // 2
                            wo_lo_part(1, c, w1_hi, WC + c + 1, wo1_lo)
                for t in range(TB):
                    if gs_slot(blk, NI + 2 * t) + 1 < R:
                        gs_factor(gs_slot(blk, NI + 2 * t) + 1)
                    inv_std(blk * TB + t)
                    if blk == BPS - 1 and t >= 2:
                        wo_lo_part(1, t - 2, w1_hi, WC + t - 1, wo1_lo)

        @block.scalar
        def _(act):
            act.wait_ge(consts, 1)
            nc.scalar.activation(act_t[:, 0:1], ident[:, 0:1], ACT.Gelu)
            act.dma_start(UV[:, 1, :, :], V.rearrange("(k p) r -> p k r", p=P)).then_inc(uv_in, 16)

            def tx_evac(blk):
                for k in range(KH):
                    act.wait_ge(tx_done, KH * blk + k + 1)
                    nc.scalar.activation(xT_hi[:, blk % 2, k, :], tp[k][:], ACT.Copy).then_inc(tx_hi, 1)

            def th_evac(blk):
                for k in range(KH):
                    act.wait_ge(th_done, KH * blk + k + 1)
                    nc.scalar.activation(hsT[:, blk, k, :], tp[k][:], ACT.Copy,
                                         accum_out=hs_sum[:, blk, k:k + 1]).then_inc(th_out, 1)

            def gelu(u):
                blk, it = divmod(u, NI)
                b = blk // BPS
                act.wait_ge(up_done, u + 1)
                if u >= UPB:
                    act.wait_ge(hlo_done, u - UPB + 1)
                bias = biT[:, b * NI + it:b * NI + it + 1]
                nc.scalar.activation(hf[:, u % UPB, :], up[u % UPB][:], ACT.Gelu, bias=bias)
                nc.scalar.activation(h_hi[:, it, :], up[u % UPB][:], ACT.Gelu, bias=bias)\
                  .then_inc(gelu_done, 1)

            def w1_part(n):
                m, c = divmod(n, WC)
                if m == 0:
                    act.wait_ge(wi_in[WC], 16)
                    o, raw = wi_cut(wi_hi, 1, c), wi_raw[:, :, c * WCUT:(c + 1) * WCUT]
                else:
                    act.wait_ge(wo_in[1], 16)
                    o, raw = wo_cut(wo_hi, 1, c), wo_raw[:, c * KCUT:(c + 1) * KCUT, :]
                nc.scalar.activation(o, raw, ACT.Copy).then_inc(w1_hi, 1)

            def proj_hi(blk):
                act.wait_ge(pj_done, blk + 1)
                nc.scalar.activation(proj[0:96, blk, :], up[blk % 2][0:96, :], ACT.Copy).then_inc(pj_hi, 1)

            def gate(b):
                act.wait_ge(z_done, 2 * b + 1)
                nc.scalar.activation(h1[:, b:b + 1], misc[0:GH, 0:1], ACT.Relu, bias=b1c[:],
                                     scale=1.0 / S).then_inc(g_act, 1)
                act.wait_ge(z_done, 2 * b + 2)
                nc.scalar.activation(act_t[:, b:b + 1], misc[:, 4:5], ACT.Tanh, bias=b2h[:],
                                     scale=0.5).then_inc(g_act, 1)

            tx_evac(0)
            for c in range(WC):
                act.wait_ge(wi_in[c], 16)
                nc.scalar.activation(wi_cut(wi_hi, 0, c), wi_raw[:, :, c * WCUT:(c + 1) * WCUT],
                                     ACT.Copy).then_inc(wi0_hi, 1)
            act.wait_ge(setup_pe, 1)
            nc.scalar.activation(biT[:], misc[:, 0:B * NI], ACT.Copy).then_inc(setup_act, 1)
            act.wait_ge(setup_act, 1)
            for blk in range(NB):
                for it in range(NI):
                    gelu(blk * NI + it)
                    if blk >= 1 and it == 5:
                        th_evac(blk - 1)
                if blk + 1 < NB:
                    tx_evac(blk + 1)
                if blk == 0:
                    act.wait_ge(gate_in, 80)
                    nc.scalar.activation(mod_t[:], sc_sb[:], ACT.Tanh, scale=0.5).then_inc(gate_act, 1)
                    act.wait_ge(setup_pe, 2)
                    nc.scalar.activation(w1T[:].rearrange("p k n -> p (k n)"), misc[:, 0:KH * GH],
                                         ACT.Copy).then_inc(setup_act, 1)
                    act.wait_ge(setup_pe, 3)
                    nc.scalar.activation(UT[:], misc[0:R, 0:H], ACT.Copy)
                    nc.scalar.activation(rwT[:], misc[0:R, H:2 * H], ACT.Copy).then_inc(setup_act, 1)
                if blk < BPS:
                    for c in range(WC):
                        w1_part(blk * WC + c)
                if blk == 2:
                    act.wait_ge(gate_dve, 1)
                    gate(0)
                if blk == 3:
                    for i in range(3):
                        proj_hi(i)
            th_evac(3)
            gate(1)
            proj_hi(3)

        @block.vector
        def _(dve):
            v = nc.vector
            seq = [0]

            def link(ins):
                seq[0] += 1
                ins.then_inc(dve_seq, 1)
                dve.wait_ge(dve_seq, seq[0])

            def tx_rest(blk):
                for k in range(KH):
                    dve.wait_ge(tx_hi, KH * blk + k + 1)
                    v.tensor_tensor(xT_lo[:, blk % 2, k, :], tp[k][:],
                                    xT_hi[:, blk % 2, k, :].bitcast(F32), ALU.subtract).then_inc(tx_lo, 1)

            def gs_old_row(i):
                if i >= 2:
                    dve.wait_ge(gsu_done, i - 1)
                v.stream_shuffle(gs_old[:, i:], gs[:, i:], [i] * R).then_inc(old_done, 1)

            def gs_keys(i):
                dve.wait_ge(f_done, i + 1)
                v.tensor_tensor(gs_k[:, i:i + 1], gs_row[:, i % 2, i + 1:i + 2], gs_f[:, i:i + 1],
                                ALU.mult).then_inc(key_done, 1)
                v.scalar_tensor_tensor(out=gs_c[:, i:i + 1], in0=gs[:, i:i + 1], scalar=gs_f[:, i:i + 1],
                                       in1=mask[:, i:i + 1], op0=ALU.mult, op1=ALU.mult)\
                 .then_inc(key_done, 1)

            def gs_eliminate(i):
                cols = slice(i + 1, R + i + 1)
                new = slice(i + 1, 2 * R)
                dve.wait_ge(key_done, 2 * i + 1)
                dve.wait_ge(old_done, i + 1)
                v.scalar_tensor_tensor(out=gs_row[:, (i + 1) % 2, new], in0=gs_row[:, i % 2, new],
                                       scalar=gs_k[:, i:i + 1], in1=gs_old[:, new],
                                       op0=ALU.mult, op1=ALU.subtract, reverse1=True).then_inc(row_done, 1)
                dve.wait_ge(key_done, 2 * i + 2)
                v.scalar_tensor_tensor(out=gs[:, cols], in0=gs_row[:, i % 2, cols],
                                       scalar=gs_c[:, i:i + 1], in1=gs[:, cols],
                                       op0=ALU.mult, op1=ALU.subtract, reverse1=True).then_inc(gsu_done, 1)

            def gs_step(i):
                if i + 1 < R:
                    gs_old_row(i + 1)
                    gs_keys(i)
                    gs_eliminate(i)

            def h_low(u):
                dve.wait_ge(gelu_done, u + 1)
                v.tensor_tensor(h_lo[:, u % NI, :], hf[:, u % UPB, :],
                                h_hi[:, u % NI, :].bitcast(F32), ALU.subtract).then_inc(hlo_done, 1)

            def ln_sum(d):
                dve.wait_ge(xb_done, d + 1)
                dve.wait_ge(down_done, d + 1)
                v.tensor_tensor(xr[:, d, :], dn[d % 2][:, 0:H], xr[:, d, :], ALU.add).then_inc(r_done, 1)

            def ln_partial(d):
                dve.wait_ge(r_done, d + 1)
                v.bn_stats(bn6[:, d, :], xr[:, d, :]).then_inc(bn_done, 1)

            def ln_moments(d):
                dve.wait_ge(bn_done, d + 1)
                v.bn_aggr(mv[:, d, :], bn6[:, d, :]).then_inc(mv_done, 1)

            def ln_guard(d):
                dve.wait_ge(mv_done, d + 1)
                v.tensor_scalar(ve[:, d:d + 1], mv[:, d, 1:2], LN_EPS, None, ALU.add).then_inc(stat_done, 1)

            def ln_gamma(d):
                dve.wait_ge(mv_done, d + 1)
                v.scalar_tensor_tensor(out=xr[:, d, :], in0=xr[:, d, :], scalar=mv[:, d, 0:1],
                                       in1=bc3[:, d // TPS, 1, :], op0=ALU.subtract, op1=ALU.mult)\
                 .then_inc(y_done, 1)

            def ln_beta(d):
                dve.wait_ge(y_done, d + 1)
                dve.wait_ge(rstd_done, d + 1)
                v.scalar_tensor_tensor(out=xr[:, d, :], in0=xr[:, d, :], scalar=rstd[:, d:d + 1],
                                       in1=bc3[:, d // TPS, 2, :], op0=ALU.mult, op1=ALU.add)\
                 .then_inc(hs_done, 1)

            def proj_rest(blk):
                dve.wait_ge(pj_hi, blk + 1)
                v.tensor_tensor(proj[64:96, blk, :], up[blk % 2][64:96, :],
                                proj[64:96, blk, :].bitcast(F32), ALU.subtract).then_inc(pj_lo, 1)

            def gate_strength(b):
                dve.wait_ge(g_act, 2 * b + 2)
                link(v.tensor_scalar(act_s[:, b:b + 1], act_t[:, b:b + 1], 0.5, 0.5, ALU.mult, ALU.add))
                v.tensor_tensor(strength[:, b:b + 1], act_s[:, b:b + 1], mod_s[:, b:b + 1], ALU.mult)\
                 .then_inc(str_done, 1)
                dve.wait_ge(str_done, b + 1)

            def final(d):
                dve.wait_ge(fin_pe, d + 1)
                v.scalar_tensor_tensor(out=xr[:, d, :], in0=resp_banks[d % 3][:, 0:H],
                                       scalar=strength[:, d // TPS:d // TPS + 1], in1=xr[:, d, :],
                                       op0=ALU.mult, op1=ALU.add).then_inc(fin_dve, 1)

            dve.wait_ge(consts, 2)
            for q in range(2):
                rows = slice(q * R, (q + 1) * R)
                v.tensor_copy(mask[rows, :], below[rows, rows])
                v.tensor_copy(eye2[rows, :], ident[rows, rows])
                v.tensor_copy(gs[rows, R:2 * R], ident[rows, rows])
            link(v.tensor_tensor(row_t[96:P, 0:1], ident[96:P, 96:97], ident[96:P, 97:98], ALU.add))
            link(v.tensor_tensor(row_m[96:P, :], ident[96:P, 98:99], ident[96:P, 99:100], ALU.add))
            link(v.tensor_tensor(row_w[96:P, :], row_t[96:P, 0:1], row_m[96:P, :], ALU.subtract))
            dve.wait_ge(gram_pe, 1)
            v.tensor_copy(gram[:], dn[0][0:2 * R, 0:R])
            link(v.tensor_copy(gs[:, 0:R], dn[0][0:2 * R, 0:R]))
            v.stream_shuffle(gs_row[:, 0, :], gs[:], [0] * R).then_inc(row_done, 1)
            for i in range(GS0):
                if i == 0:
                    dve.wait_ge(row_done, 1)
                gs_step(i)
                if i == 0:
                    tx_rest(0)
                dve.wait_ge(wi0_hi, i + 1)
                v.tensor_tensor(wi_cut(wi_lo, 0, i), wi_raw[:, :, i * WCUT:(i + 1) * WCUT],
                                wi_cut(wi_hi, 0, i).bitcast(F32), ALU.subtract).then_inc(wi0_lo, 1)

            for blk in range(NB):
                for it in range(NI):
                    u = blk * NI + it
                    if it % 2 == 0 and gs_slot(blk, it) < R:
                        gs_step(gs_slot(blk, it))
                    if blk == 0 and it < WC:
                        dve.wait_ge(wo_in[0], 16)
                        v.tensor_copy(wo_cut(wo_hi, 0, it), wo_raw[:, it * KCUT:(it + 1) * KCUT, :])\
                         .then_inc(wo0_hi, 1)
                    h_low(u)
                    if blk == 0 and WC - WO_D <= it < WC:
                        dve.wait_ge(wo0_hi, it + 1)
                        v.tensor_tensor(wo_cut(wo_lo, 0, it), wo_raw[:, it * KCUT:(it + 1) * KCUT, :],
                                        wo_cut(wo_hi, 0, it).bitcast(F32), ALU.subtract)\
                         .then_inc(wo0_lo_d, 1)
                    if blk >= 1 and it == 0:
                        ln_beta(blk * TB - 1)
                    if blk == 1 and it % 2 == 1:
                        c = it // 2
                        dve.wait_ge(w1_hi, c + 1)
                        v.tensor_tensor(wi_cut(wi_lo, 1, c), wi_raw[:, :, c * WCUT:(c + 1) * WCUT],
                                        wi_cut(wi_hi, 1, c).bitcast(F32), ALU.subtract).then_inc(wi1_lo, 1)
                if blk == 3:
                    dve.wait_ge(f_done, R)
                    dve.wait_ge(gsu_done, R - 1)
                    link(v.tensor_tensor(gs_d[:], gs_ne[:], eye2[:], ALU.mult))
                    link(v.reduce_sum(gs_dn[:], gs_d[:], axis=AX_X))
                    link(v.reciprocal(gs_rn[:], gs_dn[:]))
                    link(v.tensor_scalar(Ln[:], gs[:, R:2 * R], gs_rn[:], None, ALU.mult))
                    v.transpose(LnT[:], Ln[:]).then_inc(alg_dve, 1)
                if blk + 1 < NB:
                    tx_rest(blk + 1)
                if blk == 0:
                    dve.wait_ge(gate_act, 1)
                    v.tensor_scalar(b2h[:], b2c[:], 0.5, None, ALU.mult)
                    v.tensor_copy(w2rep[:], w2c[:].to_broadcast([GH, P]))
                    v.tensor_scalar(mod_s[:], mod_t[:], 0.5, 0.5, ALU.mult, ALU.add).then_inc(gate_dve, 1)
                for t in range(TB):
                    d = blk * TB + t
                    step = gs_slot(blk, NI + 2 * t)
                    if blk == 3 and t == 0:
                        dve.wait_ge(alg_pe, 1)
                        v.tensor_copy(gw_sb[R:2 * R, :], tp[0][R:2 * R, 0:R])
                        v.tensor_copy(uo_top[:], misc[0:R, 0:R]).then_inc(alg_dve, 1)
                        uo = misc[:, 0:KH * R].rearrange("p (k r) -> p k r", k=KH)
                        for k in range(KH):
                            last = v.tensor_copy(urep[:, k, :, :],
                                                 uo[:, k, :].unsqueeze(1).to_broadcast([P, 3, R]))
                        last.then_inc(alg_dve, 1)
                    if blk == 3 and t == 1:
                        dve.wait_ge(alg_pe, 2)
                        v.tensor_copy(vtv[:], tp[0][0:R, 0:R].unsqueeze(1).to_broadcast([R, 3, R]))
                        v.tensor_copy(ur[:], misc[0:R, 0:H]).then_inc(alg_dve, 1)
                    if blk == 3 and t == 2:
                        dve.wait_ge(alg_pe, 3)
                        link(v.tensor_copy(g_hi[0:96, :], misc[0:96, 0:H]))
                        v.tensor_copy(resp_rhs[0:R, :], g_hi[0:R, :].bitcast(F32))
                        v.tensor_copy(resp_rhs[2 * R:3 * R, :], g_hi[2 * R:3 * R, :].bitcast(F32))
                        v.tensor_tensor(resp_rhs[R:2 * R, :], misc[R:2 * R, 0:H],
                                        g_hi[R:2 * R, :].bitcast(F32), ALU.subtract).then_inc(rhs_dve, 1)
                    if blk == 3 and t == 3:
                        proj_rest(0)
                    ln_sum(d)
                    if step + 1 < R:
                        gs_old_row(step + 1)
                        gs_keys(step)
                    ln_partial(d)
                    if step + 1 < R:
                        gs_eliminate(step)
                    ln_moments(d)
                    if t >= 1:
                        ln_beta(d - 1)
                    ln_guard(d)
                    ln_gamma(d)
                    if blk == 1 and t == 0:
                        dve.wait_ge(bias_in, 64)
                        link(v.tensor_copy(g_hi[96:P, :], bias_raw[96:P, :]))
                        v.scalar_tensor_tensor(out=resp_rhs[96:P, :], in0=bias_raw[96:P, :],
                                               scalar=row_m[96:P, :], in1=g_hi[96:P, :].bitcast(F32),
                                               op0=ALU.mult, op1=ALU.subtract, reverse1=True)
                    if blk == 1 and t >= 1:
                        for i in ((0,), (1,), (2, 3))[t - 1]:
                            v.tensor_copy(proj[96:P, i, :], row_w[96:P, :].to_broadcast([R, BT]))
                if blk == 2:
                    gate_strength(0)
            ln_beta(NT - 1)
            for d in range(4):
                final(d)
                if d == 0:
                    proj_rest(1)
            proj_rest(2)
            final(4)
            final(5)
            gate_strength(1)
            for d in range(6, 10):
                final(d)
            proj_rest(3)
            for d in range(10, NT):
                final(d)

        @block.tensor
        def _(pe):
            def x_transposes(blk):
                pe.wait_ge(x_in[blk], 16)
                for k in range(KH):
                    if blk == 1:
                        pe.wait_ge(tx_lo, k + 1)
                    elif blk >= 2:
                        pe.wait_ge(th_out, KH * (blk - 2) + k + 1)
                    for t in range(TB):
                        last = nc.tensor.transpose(tp[k][:, t * P:(t + 1) * P],
                                                   xr[:, blk * TB + t, k * P:(k + 1) * P], ident[:])
                    last.then_inc(tx_done, 1)

            def hs_transposes(blk):
                pe.wait_ge(hs_done, (blk + 1) * TB)
                for k in range(KH):
                    if blk + 1 < NB:
                        pe.wait_ge(tx_lo, KH * (blk + 1) + k + 1)
                    else:
                        pe.wait_ge(alg_dve, 4)
                    for t in range(TB):
                        last = nc.tensor.transpose(tp[k][:, t * P:(t + 1) * P],
                                                   xr[:, blk * TB + t, k * P:(k + 1) * P], ident[:])
                    last.then_inc(th_done, 1)

            def up_unit(u):
                blk, it = divmod(u, NI)
                b, s = blk // BPS, blk % 2
                if u >= UPB:
                    pe.wait_ge(gelu_done, u - UPB + 1)
                if it == 0:
                    pe.wait_ge(tx_lo, KH * (blk + 1))
                if blk == 0:
                    pe.wait_ge(wi0_lo, it * WC // NI + 1)
                elif blk == BPS and it == 0:
                    pe.wait_ge(wi1_lo, WC)
                cut = slice(it * P, (it + 1) * P)
                parts = [(wi_hi, xT_hi), (wi_hi, xT_lo), (wi_lo, xT_hi)]
                for k in range(KH):
                    for n, (w, xs) in enumerate(parts):
                        last = nc.tensor.matmul(up[u % UPB][:], w[:, b, k, cut], xs[:, s, k, :],
                                                start=(k == 0 and n == 0),
                                                stop=(k == KH - 1 and n == len(parts) - 1))
                last.then_inc(up_done, 1)

            def down_tile(d):
                blk, t = divmod(d, TB)
                b = blk // BPS
                if d >= 2:
                    pe.wait_ge(r_done, d - 1)
                cut = slice(t * P, (t + 1) * P)
                parts = [(h_hi, wo_hi), (h_hi, wo_lo), (h_lo, wo_hi)]
                for k in range(NI):
                    c = k // KCUT
                    if t == 0:
                        pe.wait_ge(hlo_done, blk * NI + k + 1)
                        if blk == 0 and c < WC - WO_D:
                            pe.wait_ge(wo0_lo_p, c + 1)
                        elif blk == 0:
                            pe.wait_ge(wo0_lo_d, c - (WC - WO_D) + 1)
                        elif blk == BPS:
                            pe.wait_ge(wo1_lo, c + 1)
                    for n, (h, w) in enumerate(parts):
                        last = nc.tensor.matmul(dn[d % 2][:, 0:H], h[:, k, cut], w[:, b, k, :],
                                                start=(k == 0 and n == 0),
                                                stop=(k == NI - 1 and n == len(parts) - 1))
                    if blk == 3 and (t, k) == (0, 3):
                        pe.wait_ge(alg_dve, 1)
                        pe.wait_ge(setup_act, 3)
                        pe.wait_ge(th_out, KH * 3)
                        nc.tensor.matmul(tp[0][R:2 * R, 0:R], gram[R:2 * R, :], LnT[R:2 * R, :],
                                         start=True, stop=True)
                        for j in range(KH):
                            small = nc.tensor.matmul(misc[:, j * R:(j + 1) * R], UT[:, j * P:(j + 1) * P],
                                                     LnT[0:R, :], start=True, stop=True)
                        small.then_inc(alg_pe, 1)
                    if blk == 3 and (t, k) == (1, 3):
                        pe.wait_ge(alg_dve, 3)
                        nc.tensor.matmul(tp[0][0:R, 0:R], LnT[R:2 * R, :], gw_sb[R:2 * R, :],
                                         start=True, stop=True)
                        nc.tensor.matmul(misc[0:R, 0:H], uo_top[:], rwT[:], start=True, stop=True)\
                          .then_inc(alg_pe, 1)
                    if blk == 3 and (t, k) == (1, 7):
                        project(0)
                    if blk == 3 and (t, k) == (2, 3):
                        pe.wait_ge(alg_dve, 4)
                        nc.tensor.matmul(misc[0:96, 0:H], vtv[:].rearrange("p j r -> p (j r)"), ur[:],
                                         start=True, stop=True).then_inc(alg_pe, 1)
                    if blk == 3 and (t, k) == (3, 0):
                        project(1)
                last.then_inc(down_done, 1)

            def project(blk):
                if blk >= 2:
                    pe.wait_ge(pj_lo, blk - 1)
                pe.wait_ge(gelu_done, NB * NI)
                pe.wait_ge(th_out, KH * (blk + 1))
                for k in range(KH):
                    last = nc.tensor.matmul(up[blk % 2][0:96, :],
                                            urep[:, k, :, :].rearrange("p j r -> p (j r)"),
                                            hsT[:, blk, k, :], start=(k == 0), stop=(k == KH - 1))
                last.then_inc(pj_done, 1)

            def gate_hidden(b):
                pe.wait_ge(th_out, KH * (b * BPS + BPS))
                n = 0
                for s in range(BPS):
                    for k in range(KH):
                        last = nc.tensor.matmul(misc[0:GH, 0:1], w1T[:, k, :],
                                                hs_sum[:, b * BPS + s, k:k + 1], start=(n == 0),
                                                stop=(n == BPS * KH - 1))
                        n += 1
                last.then_inc(z_done, 1)

            def gate_out(b):
                pe.wait_ge(g_act, 2 * b + 1)
                nc.tensor.matmul(misc[:, 4:5], w2rep[:], h1[:, b:b + 1], start=True, stop=True)\
                  .then_inc(z_done, 1)

            def response(d):
                blk, t = divmod(d, TB)
                pe.wait_ge(pj_lo, blk + 1)
                if d == 0:
                    pe.wait_ge(rhs_dve, 1)
                if d in (1, 2):
                    pe.wait_ge(r_done, NT - 2 + d)
                if d >= 3:
                    pe.wait_ge(fin_dve, d - 2)
                nc.tensor.matmul(resp_banks[d % 3][:, 0:H], proj[:, blk, t * P:(t + 1) * P],
                                 resp_rhs[:], start=True, stop=True).then_inc(fin_pe, 1)

            pe.wait_ge(consts, 1)
            pe.wait_ge(uv_in, 32)
            for m in range(2):
                for k in range(KH):
                    last = nc.tensor.matmul(dn[0][m * R:(m + 1) * R, 0:R], UV[:, m, k, :], UV[:, m, k, :],
                                            start=(k == 0), stop=(k == KH - 1))
            last.then_inc(gram_pe, 1)
            x_transposes(0)
            pe.wait_ge(bi_in, 32)
            nc.tensor.transpose(misc[:, 0:B * NI], bi_sb[:], ident[0:B * NI, 0:B * NI])\
              .then_inc(setup_pe, 1)

            for blk in range(NB):
                for it in range(NI):
                    up_unit(blk * NI + it)
                    if blk >= 1 and it == 4:
                        hs_transposes(blk - 1)
                if blk + 1 < NB:
                    x_transposes(blk + 1)
                for t in range(TB):
                    if blk == 0 and t == 1:
                        pe.wait_ge(gate_in, 80)
                        pe.wait_ge(setup_act, 1)
                        for k in range(KH):
                            last = nc.tensor.transpose(misc[:, k * GH:(k + 1) * GH],
                                                       w1_sb[:, k * P:(k + 1) * P], ident[0:GH, 0:GH])
                        last.then_inc(setup_pe, 1)
                    if blk == 0 and t == 2:
                        pe.wait_ge(rw_in, 16)
                        pe.wait_ge(setup_act, 2)
                        for k in range(KH):
                            nc.tensor.transpose(misc[0:R, k * P:(k + 1) * P], UV[:, 0, k, :], ident[:])
                        for k in range(KH):
                            last = nc.tensor.transpose(misc[0:R, H + k * P:H + (k + 1) * P],
                                                       rw[:, k, :], ident[:])
                        last.then_inc(setup_pe, 1)
                    if blk == 2 and t == 1:
                        pe.wait_ge(gate_dve, 1)
                        gate_hidden(0)
                    if blk == 2 and t == 2:
                        gate_out(0)
                    down_tile(blk * TB + t)
            project(2)
            for d in range(3):
                response(d)
            hs_transposes(3)
            for d in range(3, 6):
                response(d)
            gate_hidden(1)
            gate_out(1)
            project(3)
            for d in range(6, NT):
                response(d)


_INS = ["x", "itok_B_0_7", "condB_safetyscore", "L0_cond_Wi", "L0_cond_bi", "L0_cond_Wo", "L0_cond_bo",
        "L0_cond_gamma", "L0_cond_beta", "L1_cond_U", "L1_cond_V", "L1_cond_safety_bias",
        "L1_cond_gate_w1", "L1_cond_gate_b1", "L1_cond_gate_w2", "L1_cond_gate_b2", "L1_cond_resp_w",
        "L1_cond_resp_b"]


def kernel(**inputs):
    import numpy as _np
    import concourse.bacc as _bacc
    from concourse import mybir as _mybir
    from concourse.bass_utils import run_bass_kernel_spmd as _run

    nc = _bacc.Bacc("TRN2", target_bir_lowering=False, num_devices=1)
    arrays, args = {}, []
    for name in _INS:
        a = _np.ascontiguousarray(inputs[name])
        arrays[f"in_{name}"] = a
        args.append(nc.dram_tensor(f"in_{name}", a.shape, _mybir.dt.from_np(a.dtype), kind="ExternalInput").ap())
    out = nc.dram_tensor("out_0", (B, S, H), _mybir.dt.float32, kind="ExternalOutput").ap()
    cond_seq_kernel(nc, *args, out)
    r = _run(nc, [arrays], core_ids=[0])
    return r.results[0]["out_0"]
```

```python
from contextlib import ExitStack

import concourse.bass as bass
from concourse import mybir

P = 128
F32 = mybir.dt.float32
F32R = mybir.dt.float32r
I32 = mybir.dt.int32
ALU = mybir.AluOpType
ACT = mybir.ActivationFunctionType
AX_X = mybir.AxisListType.X

B, S, H = 2, 1024, 256
E, F = 8, 1024
R = 32
GH = 64
BT = 512
NB = B * S // BT
BPS = NB // B
TB = BT // P
TPS = S // P
NT = B * TPS
KH = H // P
NI = F // P
WC = 4
UPB = 3
HFS = 5
GROUPS = tuple((b * TB, TB) for b in range(NB - 1)) + ((NT - 4, 2), (NT - 2, 2))
PROJ_ORDER = (0, 1, 3, 2, 4)
RESP_ORDER = (0, 2, 4, 6, NT - 4, NT - 8, NT - 6, NT - 2)
LN_EPS = 1e-12
GS_EPS = 1e-8


def cond_seq_kernel(nc, x, itok, score, Wi, bi, Wo, bo, gamma, beta, U, V, safety_bias,
                    gate_w1, gate_b1, gate_w2, gate_b2, resp_w, resp_b, out):
    x_v = x.rearrange("b (n p) h -> p (b n) h", p=P)
    out_v = out.rearrange("b (n p) h -> p (b n) h", p=P)
    Wi_rows = Wi.rearrange("e h i -> (e h) i")
    Wo_rows = Wo.rearrange("e i h -> (e i) h")
    bi_rows = bi.rearrange("e (a p) -> (e a) p", p=P)

    with ExitStack() as ctx:
        def sb(name, shape, dt=F32):
            return ctx.enter_context(nc.sbuf_tensor(name, shape, dt))

        def bank(name):
            return ctx.enter_context(nc.psum_tensor(name, [P, 512], F32))

        def sem(name):
            return ctx.enter_context(nc.semaphore(name))

        xr = sb("xr", [P, NT, H])
        xT_hi = sb("xT_hi", [P, 2, KH, BT], F32R)
        xT_lo = sb("xT_lo", [P, 2, KH, BT], F32R)
        wi_raw = sb("wi_raw", [P, KH, F])
        wo_raw = sb("wo_raw", [P, NI, H])
        wi_hi = sb("wi_hi", [P, B, KH, F], F32R)
        wi_lo = sb("wi_lo", [P, B, KH, F], F32R)
        wo_hi = sb("wo_hi", [P, B, NI, H], F32R)
        wo_lo = sb("wo_lo", [P, B, NI, H], F32R)
        hf = sb("hf", [P, HFS, BT])
        h_hi = sb("h_hi", [P, NI, BT], F32R)
        h_lo = sb("h_lo", [P, NI, BT], F32R)
        hsT = sb("hsT", [P, NB, KH, BT])
        hs_sum = sb("hs_sum", [P, len(GROUPS), KH])
        rows3 = sb("rows3", [1, B, 3, H])
        bc3 = sb("bc3", [P, B, 3, H])
        bi_sb = sb("bi_sb", [B * NI, P])
        biT = sb("biT", [P, B * NI])
        bn6 = sb("bn6", [P, NT, 6])
        mv = sb("mv", [P, NT, 2])
        ve = sb("ve", [P, NT])
        rstd = sb("rstd", [P, NT])
        idx = sb("idx", [1, B], I32)
        ident = sb("ident", [P, P])
        below = sb("below", [P, P])
        half_neg = sb("half_neg", [P, 1])
        half_pos = sb("half_pos", [P, 1])
        neg_two = sb("neg_two", [P, 1])
        UV = sb("UV", [P, 2, KH, R])
        rw = sb("rw", [P, KH, R])
        UT = sb("UT", [R, H])
        rwT = sb("rwT", [R, H])
        mask = sb("mask", [2 * R, R])
        eye2 = sb("eye2", [2 * R, R])
        gram = sb("gram", [2 * R, R])
        gs = sb("gs", [2 * R, 2 * R])
        gs_row = sb("gs_row", [2 * R, 2, 2 * R])
        gs_n = sb("gs_n", [2 * R, R])
        gs_ne = sb("gs_ne", [2 * R, R])
        gs_f = sb("gs_f", [2 * R, R])
        ones = sb("ones", [P, 1])
        scaled = sb("scaled", [P, 2, H])
        gs_c = sb("gs_c", [2 * R, R])
        gs_d = sb("gs_d", [2 * R, R])
        gs_dn = sb("gs_dn", [2 * R, 1])
        gs_rn = sb("gs_rn", [2 * R, 1])
        Ln = sb("Ln", [2 * R, R])
        LnT = sb("LnT", [2 * R, R])
        gw_sb = sb("gw_sb", [2 * R, R])
        uo_top = sb("uo_top", [R, R])
        urep = sb("urep", [P, KH, 3, R])
        vtv = sb("vtv", [R, 3, R])
        ur = sb("ur", [R, H])
        g_hi = sb("g_hi", [P, H], F32R)
        resp_rhs = sb("resp_rhs", [P, H], F32R)
        bias_raw = sb("bias_raw", [P, H])
        row_w = sb("row_w", [P, 1])
        row_m = sb("row_m", [P, 1])
        row_t = sb("row_t", [P, 2])
        proj = sb("proj", [P, NT * P], F32R)
        w1_sb = sb("w1_sb", [GH, H])
        w1T = sb("w1T", [P, KH, GH])
        b1c = sb("b1c", [GH, 1])
        w2c = sb("w2c", [GH, 1])
        w2rep = sb("w2rep", [GH, P])
        b2c = sb("b2c", [P, 1])
        b2h = sb("b2h", [P, 1])
        sc_sb = sb("sc_sb", [P, B])
        mod_t = sb("mod_t", [P, B])
        mod_s = sb("mod_s", [P, B])
        h1 = sb("h1", [GH, B])
        act_t = sb("act_t", [P, B])
        act_s = sb("act_s", [P, B])
        strength = sb("strength", [P, B])

        up = [bank(f"up{i}") for i in range(UPB)]
        dn = [bank(f"dn{i}") for i in range(2)]
        tp = [bank(f"tp{i}") for i in range(2)]
        misc = bank("misc")

        idx_in = sem("idx_in")
        x_in = [sem(f"x_in{i}") for i in range(NB)]
        wi_in = [sem(f"wi_in{i}") for i in range(WC + 1)]
        wo_in = [sem(f"wo_in{i}") for i in range(B)]
        bi_in = sem("bi_in")
        rows_in = [sem(f"rows_in{i}") for i in range(B)]
        uv_in = sem("uv_in")
        rw_in = sem("rw_in")
        gate_in = sem("gate_in")
        bias_in = sem("bias_in")
        out_done = sem("out_done")
        consts = sem("consts")
        gram_pe = sem("gram_pe")
        setup_pe = sem("setup_pe")
        setup_act = sem("setup_act")
        weights_done = sem("weights_done")
        rows_act = sem("rows_act")
        gate_act = sem("gate_act")
        gate_dve = sem("gate_dve")
        tx_done = sem("tx_done")
        tx_hi = sem("tx_hi")
        tx_lo = sem("tx_lo")
        th_done = sem("th_done")
        th_out = sem("th_out")
        wi0_hi = sem("wi0_hi")
        wi0_lo = sem("wi0_lo")
        wo0_hi = sem("wo0_hi")
        wo0_lo_d = sem("wo0_lo_d")
        wo0_lo_p = sem("wo0_lo_p")
        w1_hi = sem("w1_hi")
        wi1_lo = sem("wi1_lo")
        wi1_lo_p = sem("wi1_lo_p")
        wo1_lo = sem("wo1_lo")
        wo1_lo_p = sem("wo1_lo_p")
        up_done = sem("up_done")
        gelu_done = sem("gelu_done")
        hlo_done = sem("hlo_done")
        down_done = sem("down_done")
        r_done = sem("r_done")
        bc_done = sem("bc_done")
        xb_done = sem("xb_done")
        bn_done = sem("bn_done")
        mv_done = sem("mv_done")
        stat_done = sem("stat_done")
        rstd_done = sem("rstd_done")
        y_done = sem("y_done")
        hs_done = sem("hs_done")
        key_done = sem("key_done")
        row_done = sem("row_done")
        f_done = sem("f_done")
        gsu_done = sem("gsu_done")
        norms_in = sem("norms_in")
        norm_done = sem("norm_done")
        alg_pe = sem("alg_pe")
        alg_dve = sem("alg_dve")
        rhs_dve = sem("rhs_dve")
        pj_done = sem("pj_done")
        pj_hi = sem("pj_hi")
        pj_lo = sem("pj_lo")
        z_done = sem("z_done")
        g_act = sem("g_act")
        str_done = sem("str_done")
        sum_pe = sem("sum_pe")
        sum_dve = sem("sum_dve")
        fin_pe = sem("fin_pe")
        fin_dve = sem("fin_dve")
        fin_act = sem("fin_act")
        fin_pool = sem("fin_pool")
        dve_seq = sem("dve_seq")
        pool_seq = sem("pool_seq")

        block = ctx.enter_context(nc.Block())

        WCUT = F // WC
        KCUT = NI // WC
        WD = 2
        POOL_CHUNK = 3
        resp_banks = [up[2], misc, up[2], misc, up[2], dn[0], dn[1], tp[1]]
        POOL_PAIR = len(RESP_ORDER) - 2
        sum_banks = [tp[1], dn[1]]
        WARM = 9

        GS_UNITS = ((0, 2, 4, 7), (1, 3, 5, 7), (1, 3, 5, 7), (0, 2, 4, 6))
        gs_places = [(0, "start", 0)]
        for blk in range(NB):
            gs_places += [(blk, "up", it) for it in GS_UNITS[blk]]
            gs_places += [(blk, "turn", 0)] + [(blk, "down", t) for t in range(TB)]
        gs_at = {place: i for i, place in enumerate(gs_places) if i < R}

        def wi_cut(t, b, c):
            return t[:, b, :, c * WCUT:(c + 1) * WCUT]

        def wo_cut(t, b, c):
            return t[:, b, c * KCUT:(c + 1) * KCUT, :]

        @block.sync
        def _(sp):
            sp.dma_start(idx[:], itok.rearrange("(a n) -> a n", a=1)).then_inc(idx_in, 16)
            sp.dma_start(xr[:, 0:TB, :], x_v[:, 0:TB, :]).then_inc(x_in[0], 16)
            sp.dma_start(UV[:, 0, :, :], U.rearrange("(k p) r -> p k r", p=P)).then_inc(uv_in, 16)
            sp.wait_ge(idx_in, 16)
            e = [sp.value_load(idx[0:1, 0:1], min_val=0, max_val=E - 1)]

            def wi_of(b):
                return Wi_rows[bass.ds(e[b] * H, H), :].rearrange("(k p) i -> p k i", p=P)

            def wo_of(b):
                return Wo_rows[bass.ds(e[b] * F, F), :].rearrange("(k p) h -> p k h", p=P)

            def rows_of(b):
                for j, src in enumerate((bo, gamma, beta)):
                    sp.dma_start(rows3[0:1, b, j, :], src[bass.ds(e[b], 1), :]).then_inc(rows_in[b], 16)

            for c in range(WC):
                cut = slice(c * WCUT, (c + 1) * WCUT)
                sp.dma_start(wi_raw[:, :, cut], wi_of(0)[:, :, cut]).then_inc(wi_in[c], 16)
                if c == 0:
                    e += [sp.value_load(idx[0:1, b:b + 1], min_val=0, max_val=E - 1) for b in range(1, B)]
                    for b in range(B):
                        sp.dma_start(bi_sb[b * NI:(b + 1) * NI, :],
                                     bi_rows[bass.ds(e[b] * NI, NI), :]).then_inc(bi_in, 16)
            rows_of(0)
            sp.dma_start(wo_raw[:], wo_of(0)).then_inc(wo_in[0], 16)
            sp.dma_start(xr[:, TB:2 * TB, :], x_v[:, TB:2 * TB, :]).then_inc(x_in[1], 16)
            sp.dma_start(w1_sb[:], gate_w1).then_inc(gate_in, 16)
            sp.dma_start(b1c[:], gate_b1.rearrange("(n a) -> n a", a=1)).then_inc(gate_in, 16)
            sp.dma_start(w2c[:], gate_w2.rearrange("a n -> n a")).then_inc(gate_in, 16)
            sp.dma_start(b2c[:], gate_b2.rearrange("(a n) -> a n", a=1).to_broadcast([P, 1])).then_inc(gate_in, 16)
            sp.dma_start(sc_sb[:], score.rearrange("(a n) -> a n", a=1).to_broadcast([P, B])).then_inc(gate_in, 16)
            sp.dma_start(rw[:], resp_w.rearrange("(k p) r -> p k r", p=P)).then_inc(rw_in, 16)
            rows_of(1)
            sp.wait_ge(consts, 3)
            for j, src in enumerate((resp_b, safety_bias, resp_b, safety_bias)):
                sp.dma_start(bias_raw[96 + j:97 + j, :],
                             src.rearrange("(a n) -> a n", a=1)).then_inc(bias_in, 16)
            sp.wait_ge(wi0_hi, WC)
            sp.wait_ge(wi0_lo, WC)
            sp.dma_start(wi_raw[:], wi_of(1)).then_inc(wi_in[WC], 16)
            for i in range(2, NB):
                sp.dma_start(xr[:, i * TB:(i + 1) * TB, :],
                             x_v[:, i * TB:(i + 1) * TB, :]).then_inc(x_in[i], 16)
            sp.wait_ge(wo0_hi, WC)
            sp.wait_ge(wo0_lo_d, WD)
            sp.wait_ge(wo0_lo_p, WC - WD)
            sp.dma_start(wo_raw[:], wo_of(1)).then_inc(wo_in[1], 16)
            for j, d in enumerate(RESP_ORDER):
                if j == POOL_PAIR:
                    sp.wait_ge(fin_pool, 1)
                else:
                    sp.wait_ge(fin_dve, j + 1 - (j > POOL_PAIR))
                sp.dma_start(out_v[:, d:d + 2, :], xr[:, d:d + 2, :]).then_inc(out_done, 16)
            n = 16 * len(RESP_ORDER)
            sp.wait_ge(out_done, n)

        @block.gpsimd
        def _(pool):
            g = nc.gpsimd
            count = {}

            def finish(ins, done=pool_seq):
                count[done.name] = count.get(done.name, 0) + 1
                ins.then_inc(done, 1)
                pool.wait_ge(done, count[done.name])

            finish(g.memset(ident[:], 0.0))
            finish(g.affine_select(out=ident[:], in_=ident[:], compare_op=ALU.not_equal, fill=1.0, base=0,
                                   pattern=[[-1, P]], channel_multiplier=1), consts)
            finish(g.memset(below[:], 1.0))
            finish(g.affine_select(out=below[:], in_=below[:], compare_op=ALU.is_gt, fill=0.0, base=0,
                                   pattern=[[-1, P]], channel_multiplier=1), consts)
            finish(g.memset(half_pos[:], 0.5))
            finish(g.memset(ones[:], 1.0))
            finish(g.memset(half_neg[:], -0.5))
            finish(g.memset(neg_two[:], -2.0))
            finish(g.memset(bias_raw[:], 0.0), consts)

            def gs_factor(i):
                pool.wait_ge(row_done, i + 1)
                d = gs_row[:, i % 2, i:i + 1]
                last = i == R - 1
                finish(g.tensor_tensor(gs_n[:, i:i + 1], d, half_pos[0:2 * R, :], ALU.pow))
                finish(g.tensor_scalar(gs_ne[:, i:i + 1], gs_n[:, i:i + 1], GS_EPS, None, ALU.add),
                       norms_in if last else pool_seq)
                if not last:
                    finish(g.tensor_tensor(gs_f[:, i:i + 1], gs_ne[:, i:i + 1], neg_two[0:2 * R, :],
                                           ALU.pow), f_done)

            def wo_lo_part(b, c, hi_done, n, done):
                pool.wait_ge(hi_done, n)
                finish(g.tensor_tensor(wo_cut(wo_lo, b, c), wo_raw[:, c * KCUT:(c + 1) * KCUT, :],
                                       wo_cut(wo_hi, b, c).bitcast(F32), ALU.subtract), done)

            def wi_lo_part():
                c = POOL_CHUNK
                pool.wait_ge(w1_hi, c + 1)
                finish(g.tensor_tensor(wi_cut(wi_lo, 1, c), wi_raw[:, :, c * WCUT:(c + 1) * WCUT],
                                       wi_cut(wi_hi, 1, c).bitcast(F32), ALU.subtract), wi1_lo_p)

            def spread_rows(b):
                pool.wait_ge(rows_in[b], 48)
                finish(g.partition_broadcast(bc3[:, b, :, :].rearrange("p j h -> p (j h)"),
                                             rows3[0:1, b, :, :].rearrange("p j h -> p (j h)")), bc_done)

            def add_bo(d):
                if d % TB == 0:
                    pool.wait_ge(tx_done, KH * (d // TB + 1))
                finish(g.tensor_tensor(xr[:, d, :], xr[:, d, :], bc3[:, d // TPS, 0, :], ALU.add), xb_done)

            def inv_std(d):
                pool.wait_ge(stat_done, d + 1)
                finish(g.tensor_tensor(rstd[:, d:d + 1], ve[:, d:d + 1], half_neg[:], ALU.pow), rstd_done)

            def gs_next(blk, phase, n):
                i = gs_at.get((blk, phase, n), R)
                if i + 1 < R:
                    gs_factor(i + 1)

            gs_factor(0)
            gs_next(0, "start", 0)
            spread_rows(0)
            for blk in range(NB):
                if blk == 1:
                    wi_lo_part()
                if blk == BPS:
                    wo_lo_part(1, POOL_CHUNK, w1_hi, WC + POOL_CHUNK + 1, wo1_lo_p)
                for it in range(NI):
                    gs_next(blk, "up", it)
                    if blk == 0:
                        if it == 0:
                            add_bo(0)
                        elif it in (3, 5):
                            c = (it - 3) // 2
                            wo_lo_part(0, c, wo0_hi, c + 1, wo0_lo_p)
                        elif it == 6:
                            add_bo(1)
                            add_bo(2)
                        elif it == 7:
                            add_bo(3)
                    elif it % 2 == 1:
                        add_bo(blk * TB + it // 2)
                gs_next(blk, "turn", 0)
                for t in range(TB):
                    if t == TB - 1:
                        inv_std(blk * TB + t)
                    gs_next(blk, "down", t)
                    if t < TB - 1:
                        inv_std(blk * TB + t)
                    if blk == BPS - 1 and t == 0:
                        spread_rows(1)
            d = RESP_ORDER[POOL_PAIR]
            pool.wait_ge(fin_act, 1)
            finish(g.tensor_tensor(xr[:, d:d + 2, :], scaled[:], xr[:, d:d + 2, :], ALU.add), fin_pool)

        @block.scalar
        def _(act):
            act.wait_ge(consts, 1)
            nc.scalar.activation(act_t[:, 0:1], ident[:, 0:1], ACT.Gelu)
            act.dma_start(UV[:, 1, :, :], V.rearrange("(k p) r -> p k r", p=P)).then_inc(uv_in, 16)

            def tx_evac(blk, k):
                act.wait_ge(tx_done, KH * blk + k + 1)
                nc.scalar.activation(xT_hi[:, blk % 2, k, :], tp[k][:], ACT.Copy).then_inc(tx_hi, 1)

            def th_evac(g):
                d, n = GROUPS[g]
                blk, t = divmod(d, TB)
                o = hsT[:, blk, :, t * P:(t + n) * P]
                if g == len(GROUPS) - 1:
                    act.wait_ge(th_done, KH * g + 1)
                    nc.scalar.activation(o, tp[0][:, 0:KH * n * P].rearrange("p (k t) -> p k t", k=KH),
                                         ACT.Copy).then_inc(th_out, 1)
                    return
                for k in range(KH):
                    act.wait_ge(th_done, KH * g + k + 1)
                    nc.scalar.activation(o[:, k, :], tp[k][:, 0:n * P], ACT.Copy,
                                         accum_out=hs_sum[:, g, k:k + 1]).then_inc(th_out, 1)

            def gelu(u):
                blk, it = divmod(u, NI)
                b = blk // BPS
                act.wait_ge(up_done, u + 1)
                if u >= HFS:
                    act.wait_ge(hlo_done, u - HFS + 1)
                bias = biT[:, b * NI + it:b * NI + it + 1]
                nc.scalar.activation(hf[:, u % HFS, :], up[u % UPB][:], ACT.Gelu, bias=bias)
                nc.scalar.activation(h_hi[:, it, :], up[u % UPB][:], ACT.Gelu, bias=bias)\
                  .then_inc(gelu_done, 1)

            def w1_part(n):
                m, c = divmod(n, WC)
                if m == 0:
                    act.wait_ge(wi_in[WC], 16)
                    o, raw = wi_cut(wi_hi, 1, c), wi_raw[:, :, c * WCUT:(c + 1) * WCUT]
                else:
                    act.wait_ge(wo_in[1], 16)
                    o, raw = wo_cut(wo_hi, 1, c), wo_raw[:, c * KCUT:(c + 1) * KCUT, :]
                nc.scalar.activation(o, raw, ACT.Copy).then_inc(w1_hi, 1)

            def proj_hi(j):
                d, n = GROUPS[PROJ_ORDER[j]]
                act.wait_ge(pj_done, j + 1)
                nc.scalar.activation(proj[0:96, d * P:(d + n) * P], up[j % 2][0:96, 0:n * P],
                                     ACT.Copy).then_inc(pj_hi, 1)

            def gate_relu(b):
                act.wait_ge(z_done, 2 * b + 1)
                nc.scalar.activation(h1[:, b:b + 1], misc[0:GH, 4:5], ACT.Relu, bias=b1c[:],
                                     scale=1.0 / S).then_inc(g_act, 1)

            def gate_tanh(b):
                act.wait_ge(z_done, 2 * b + 2)
                nc.scalar.activation(act_t[:, b:b + 1], misc[:, 8:9], ACT.Tanh, bias=b2h[:],
                                     scale=0.5).then_inc(g_act, 1)

            def w0_part(c):
                act.wait_ge(wi_in[c], 16)
                nc.scalar.activation(wi_cut(wi_hi, 0, c), wi_raw[:, :, c * WCUT:(c + 1) * WCUT],
                                     ACT.Copy).then_inc(wi0_hi, 1)

            tx_evac(0, 0)
            w0_part(0)
            tx_evac(0, 1)
            w0_part(1)
            act.wait_ge(setup_pe, 1)
            nc.scalar.activation(biT[:], misc[:, 0:B * NI], ACT.Copy).then_inc(setup_act, 1)
            w0_part(2)
            act.wait_ge(setup_act, 1)
            for blk in range(NB):
                for it in range(NI):
                    gelu(blk * NI + it)
                    if blk == 0 and it + 3 < WC:
                        w0_part(it + 3)
                if blk + 1 < NB:
                    for k in range(KH):
                        tx_evac(blk + 1, k)
                if blk < BPS:
                    for c in range(WC):
                        w1_part(blk * WC + c)
                if blk == 0:
                    act.wait_ge(gate_in, 80)
                    nc.scalar.activation(mod_t[:], sc_sb[:], ACT.Tanh, scale=0.5).then_inc(gate_act, 1)
                    act.wait_ge(setup_pe, 2)
                    nc.scalar.activation(w1T[:].rearrange("p k n -> p (k n)"), misc[:, 0:KH * GH],
                                         ACT.Copy).then_inc(setup_act, 1)
                    act.wait_ge(setup_pe, 3)
                    nc.scalar.activation(UT[:], misc[0:R, 0:H], ACT.Copy)
                    nc.scalar.activation(rwT[:], misc[0:R, H:2 * H], ACT.Copy).then_inc(setup_act, 1)
                if blk == 1:
                    act.wait_ge(weights_done, 1)
                    for i in range(NB):
                        last = nc.scalar.activation(proj[96:P, i * BT:(i + 1) * BT],
                                                    row_w[96:P, :].to_broadcast([R, BT]), ACT.Copy)
                    last.then_inc(rows_act, 1)
                if blk == NB - 1:
                    proj_hi(0)
                if blk >= 1:
                    th_evac(blk - 1)
                if blk == 2:
                    act.wait_ge(gate_dve, 1)
                    gate_relu(0)
                    gate_tanh(0)
            proj_hi(1)
            th_evac(3)
            proj_hi(2)
            proj_hi(3)
            gate_relu(1)
            th_evac(4)
            gate_tanh(1)
            act.wait_ge(fin_pe, POOL_PAIR + 1)
            act.wait_ge(str_done, 2)
            nc.scalar.activation(scaled[:].rearrange("p t h -> p (t h)"), resp_banks[POOL_PAIR][:],
                                 ACT.Copy, scale=strength[:, 1:2]).then_inc(fin_act, 1)
            proj_hi(4)

        @block.vector
        def _(dve):
            v = nc.vector
            seq = [0]

            def link(ins):
                seq[0] += 1
                ins.then_inc(dve_seq, 1)
                dve.wait_ge(dve_seq, seq[0])

            def tx_rest(blk, k):
                dve.wait_ge(tx_hi, KH * blk + k + 1)
                v.tensor_tensor(xT_lo[:, blk % 2, k, :], tp[k][:],
                                xT_hi[:, blk % 2, k, :].bitcast(F32), ALU.subtract).then_inc(tx_lo, 1)

            def wi_rest(b, c, done):
                v.tensor_tensor(wi_cut(wi_lo, b, c), wi_raw[:, :, c * WCUT:(c + 1) * WCUT],
                                wi_cut(wi_hi, b, c).bitcast(F32), ALU.subtract).then_inc(done, 1)

            def wo_rest(b, c, done):
                v.tensor_tensor(wo_cut(wo_lo, b, c), wo_raw[:, c * KCUT:(c + 1) * KCUT, :],
                                wo_cut(wo_hi, b, c).bitcast(F32), ALU.subtract).then_inc(done, 1)

            def w1_rest(n):
                m, c = divmod(n, WC)
                dve.wait_ge(w1_hi, n + 1)
                (wi_rest, wo_rest)[m](1, c, (wi1_lo, wo1_lo)[m])

            def gs_spread(i):
                if i < R:
                    if i > 0:
                        dve.wait_ge(gsu_done, i)
                    v.stream_shuffle(gs_row[:, i % 2, i:], gs[:, i:], [i] * R).then_inc(row_done, 1)

            def gs_keys(i):
                if i + 1 < R:
                    dve.wait_ge(f_done, i + 1)
                    v.scalar_tensor_tensor(out=gs_c[:, i:i + 1], in0=gs[:, i:i + 1],
                                           scalar=gs_f[:, i:i + 1], in1=mask[:, i:i + 1],
                                           op0=ALU.mult, op1=ALU.mult).then_inc(key_done, 1)

            def gs_eliminate(i):
                if i + 1 < R:
                    cols = slice(i + 1, R + i + 1)
                    dve.wait_ge(key_done, i + 1)
                    v.scalar_tensor_tensor(out=gs[:, cols], in0=gs_row[:, i % 2, cols],
                                           scalar=gs_c[:, i:i + 1], in1=gs[:, cols],
                                           op0=ALU.mult, op1=ALU.subtract, reverse1=True)\
                     .then_inc(gsu_done, 1)

            def gs_step(i):
                gs_keys(i)
                gs_eliminate(i)
                gs_spread(i + 1)

            def h_low(u):
                dve.wait_ge(gelu_done, u + 1)
                v.tensor_tensor(h_lo[:, u % NI, :], hf[:, u % HFS, :],
                                h_hi[:, u % NI, :].bitcast(F32), ALU.subtract).then_inc(hlo_done, 1)

            def ln_sum(d):
                dve.wait_ge(xb_done, d + 1)
                dve.wait_ge(down_done, d + 1)
                v.tensor_tensor(xr[:, d, :], dn[d % 2][:, 0:H], xr[:, d, :], ALU.add).then_inc(r_done, 1)

            def ln_partial(d):
                dve.wait_ge(r_done, d + 1)
                v.bn_stats(bn6[:, d, :], xr[:, d, :]).then_inc(bn_done, 1)

            def ln_moments(d):
                dve.wait_ge(bn_done, d + 1)
                v.bn_aggr(mv[:, d, :], bn6[:, d, :]).then_inc(mv_done, 1)

            def ln_guard(d):
                dve.wait_ge(mv_done, d + 1)
                v.tensor_scalar(ve[:, d:d + 1], mv[:, d, 1:2], LN_EPS, None, ALU.add).then_inc(stat_done, 1)

            def ln_gamma(d):
                dve.wait_ge(mv_done, d + 1)
                v.scalar_tensor_tensor(out=xr[:, d, :], in0=xr[:, d, :], scalar=mv[:, d, 0:1],
                                       in1=bc3[:, d // TPS, 1, :], op0=ALU.subtract, op1=ALU.mult)\
                 .then_inc(y_done, 1)

            def ln_beta(d):
                dve.wait_ge(y_done, d + 1)
                dve.wait_ge(rstd_done, d + 1)
                v.scalar_tensor_tensor(out=xr[:, d, :], in0=xr[:, d, :], scalar=rstd[:, d:d + 1],
                                       in1=bc3[:, d // TPS, 2, :], op0=ALU.mult, op1=ALU.add)\
                 .then_inc(hs_done, 1)

            def proj_rest(j):
                d, n = GROUPS[PROJ_ORDER[j]]
                o = proj[64:96, d * P:(d + n) * P]
                dve.wait_ge(pj_hi, j + 1)
                v.tensor_tensor(o, up[j % 2][64:96, 0:n * P], o.bitcast(F32), ALU.subtract)\
                 .then_inc(pj_lo, 1)

            def gate_strength(b):
                dve.wait_ge(g_act, 2 * b + 2)
                link(v.tensor_scalar(act_s[:, b:b + 1], act_t[:, b:b + 1], 0.5, 0.5, ALU.mult, ALU.add))
                v.tensor_tensor(strength[:, b:b + 1], act_s[:, b:b + 1], mod_s[:, b:b + 1], ALU.mult)\
                 .then_inc(str_done, 1)
                dve.wait_ge(str_done, b + 1)

            def final(j):
                d = RESP_ORDER[j]
                dve.wait_ge(fin_pe, j + 1)
                tiles = xr[:, d:d + 2, :].rearrange("p t h -> p (t h)")
                v.scalar_tensor_tensor(out=tiles, in0=resp_banks[j][:],
                                       scalar=strength[:, d // TPS:d // TPS + 1], in1=tiles,
                                       op0=ALU.mult, op1=ALU.add).then_inc(fin_dve, 1)

            dve.wait_ge(consts, 2)
            for q in range(2):
                rows = slice(q * R, (q + 1) * R)
                v.tensor_copy(mask[rows, :], below[rows, rows])
                v.tensor_copy(eye2[rows, :], ident[rows, rows])
                v.tensor_copy(gs[rows, R:2 * R], ident[rows, rows])
            link(v.tensor_tensor(row_t[96:P, 0:1], ident[96:P, 96:97], ident[96:P, 97:98], ALU.add))
            link(v.tensor_tensor(row_m[96:P, :], ident[96:P, 98:99], ident[96:P, 99:100], ALU.add))
            v.tensor_tensor(row_w[96:P, :], row_t[96:P, 0:1], row_m[96:P, :], ALU.subtract)\
             .then_inc(weights_done, 1)
            dve.wait_ge(gram_pe, 1)
            v.tensor_copy(gram[:], dn[0][0:2 * R, 0:R])
            link(v.tensor_copy(gs[:, 0:R], dn[0][0:2 * R, 0:R]))
            gs_spread(0)
            tx_rest(0, 0)
            dve.wait_ge(wi0_hi, 1)
            wi_rest(0, 0, wi0_lo)
            tx_rest(0, 1)
            gs_step(0)
            for c in (1, 2):
                dve.wait_ge(wi0_hi, c + 1)
                wi_rest(0, c, wi0_lo)

            for blk in range(NB):
                for it in range(NI):
                    u = blk * NI + it
                    if blk == 0 and 2 <= it < 2 + WC:
                        if it == 2:
                            dve.wait_ge(wo_in[0], 16)
                        c = it - 2
                        v.tensor_copy(wo_cut(wo_hi, 0, c), wo_raw[:, c * KCUT:(c + 1) * KCUT, :])\
                         .then_inc(wo0_hi, 1)
                    h_low(u)
                    if blk == 0 and it + 3 < WC:
                        dve.wait_ge(wi0_hi, it + 4)
                        wi_rest(0, it + 3, wi0_lo)
                    if blk == 0 and it >= NI - WD:
                        c = it - NI + WC
                        dve.wait_ge(wo0_hi, c + 1)
                        wo_rest(0, c, wo0_lo_d)
                    if (blk, "up", it) in gs_at:
                        gs_step(gs_at[blk, "up", it])
                    if blk >= 1 and it == 1:
                        ln_beta(blk * TB - 1)
                    if blk == NB - 1 and it == NI - 2:
                        dve.wait_ge(norms_in, 1)
                        v.tensor_tensor(gs_d[:], gs_ne[:], eye2[:], ALU.mult).then_inc(norm_done, 1)
                    if blk == NB - 1 and it == NI - 1:
                        dve.wait_ge(norm_done, 1)
                        v.reduce_sum(gs_dn[:], gs_d[:], axis=AX_X).then_inc(norm_done, 1)
                        dve.wait_ge(norm_done, 2)
                        v.reciprocal(gs_rn[:], gs_dn[:]).then_inc(norm_done, 1)
                        dve.wait_ge(norm_done, 3)
                        v.tensor_scalar(Ln[:], gs[:, R:2 * R], gs_rn[:], None, ALU.mult)\
                         .then_inc(norm_done, 1)
                        dve.wait_ge(norm_done, 4)
                        v.transpose(LnT[:], Ln[:]).then_inc(alg_dve, 1)
                if blk + 1 < NB:
                    for k in range(KH):
                        tx_rest(blk + 1, k)
                if (blk, "turn", 0) in gs_at:
                    gs_step(gs_at[blk, "turn", 0])
                for t in range(TB):
                    d = blk * TB + t
                    step = gs_at.get((blk, "down", t), R)
                    if blk == 3 and t == 0:
                        dve.wait_ge(alg_pe, 1)
                        v.tensor_copy(gw_sb[R:2 * R, :], up[2][R:2 * R, 0:R])
                        v.tensor_copy(uo_top[:], misc[0:R, 0:R]).then_inc(alg_dve, 1)
                        uo = misc[:, 0:KH * R].rearrange("p (k r) -> p k r", k=KH)
                        for k in range(KH):
                            last = v.tensor_copy(urep[:, k, :, :],
                                                 uo[:, k, :].unsqueeze(1).to_broadcast([P, 3, R]))
                        last.then_inc(alg_dve, 1)
                    if blk == 3 and t == 1:
                        dve.wait_ge(alg_pe, 2)
                        v.tensor_copy(vtv[:], up[2][0:R, 0:R].unsqueeze(1).to_broadcast([R, 3, R]))
                        v.tensor_copy(ur[:], misc[0:R, 0:H]).then_inc(alg_dve, 1)
                        dve.wait_ge(alg_pe, 3)
                        link(v.tensor_copy(g_hi[0:96, :], misc[0:96, 0:H]))
                        v.tensor_copy(resp_rhs[0:R, :], g_hi[0:R, :].bitcast(F32))
                        v.tensor_copy(resp_rhs[2 * R:3 * R, :], g_hi[2 * R:3 * R, :].bitcast(F32))
                        v.tensor_tensor(resp_rhs[R:2 * R, :], misc[R:2 * R, 0:H],
                                        g_hi[R:2 * R, :].bitcast(F32), ALU.subtract).then_inc(rhs_dve, 1)
                    if blk == 3 and t >= 2:
                        final(2 * t - 4)
                        final(2 * t - 3)
                    if blk == 3 and t >= 1:
                        proj_rest(t - 1)
                    ln_sum(d)
                    gs_keys(step)
                    ln_partial(d)
                    gs_eliminate(step)
                    ln_moments(d)
                    gs_spread(step + 1)
                    if blk < 3 and t >= 1:
                        ln_beta(d - 1)
                    ln_guard(d)
                    ln_gamma(d)
                    if blk == 3:
                        ln_beta(d)
                    c = t - 1
                    if blk < BPS and 0 <= c < POOL_CHUNK:
                        w1_rest(blk * WC + c)
                    if blk == 2 and t == 2:
                        dve.wait_ge(bias_in, 64)
                        link(v.tensor_copy(g_hi[96:P, :], bias_raw[96:P, :]))
                        v.scalar_tensor_tensor(out=resp_rhs[96:P, :], in0=bias_raw[96:P, :],
                                               scalar=row_m[96:P, :], in1=g_hi[96:P, :].bitcast(F32),
                                               op0=ALU.mult, op1=ALU.subtract, reverse1=True)
                if blk == 0:
                    dve.wait_ge(gate_act, 1)
                    v.tensor_scalar(b2h[:], b2c[:], 0.5, None, ALU.mult)
                    v.tensor_copy(w2rep[:], w2c[:].to_broadcast([GH, P]))
                    v.tensor_scalar(mod_s[:], mod_t[:], 0.5, 0.5, ALU.mult, ALU.add).then_inc(gate_dve, 1)
                if blk == 2:
                    gate_strength(0)
            dve.wait_ge(sum_pe, 1)
            for k in range(KH):
                v.tensor_copy(hs_sum[:, len(GROUPS) - 1, k:k + 1], sum_banks[k][:, 0:1]).then_inc(sum_dve, 1)
            proj_rest(3)
            gate_strength(1)
            final(4)
            final(5)
            proj_rest(4)
            final(7)

        @block.tensor
        def _(pe):
            def keep_warm(n):
                for _ in range(n):
                    nc.tensor.matmul(up[0][:, 0:P], ident[:], ident[:], start=True, stop=True)

            def x_transposes(blk, k):
                pe.wait_ge(x_in[blk], 16)
                if blk in (1, 2):
                    pe.wait_ge(tx_lo, KH * (blk - 1) + k + 1)
                elif blk >= 3:
                    pe.wait_ge(th_out, KH * (blk - 3) + k + 1)
                for t in range(TB):
                    last = nc.tensor.transpose(tp[k][:, t * P:(t + 1) * P],
                                               xr[:, blk * TB + t, k * P:(k + 1) * P], ident[:])
                last.then_inc(tx_done, 1)

            def hs_transposes(g):
                d, n = GROUPS[g]
                pe.wait_ge(hs_done, d + n)
                for k in range(KH):
                    if g + 2 < NB:
                        pe.wait_ge(tx_lo, KH * (g + 2) + k + 1)
                    else:
                        pe.wait_ge(th_out, KH * (g - 1) + k + 1)
                    for t in range(n):
                        last = nc.tensor.transpose(tp[k][:, t * P:(t + 1) * P],
                                                   xr[:, d + t, k * P:(k + 1) * P], ident[:])
                    last.then_inc(th_done, 1)

            def last_transposes(t):
                d, n = GROUPS[-1]
                pe.wait_ge(hs_done, d + t + 1)
                pe.wait_ge(th_out, KH * (len(GROUPS) - 1))
                for k in range(KH):
                    last = nc.tensor.transpose(tp[0][:, (k * n + t) * P:(k * n + t + 1) * P],
                                               xr[:, d + t, k * P:(k + 1) * P], ident[:])
                if t == n - 1:
                    last.then_inc(th_done, 1)

            def up_unit(u):
                blk, it = divmod(u, NI)
                b, s = blk // BPS, blk % 2
                if u >= UPB:
                    pe.wait_ge(gelu_done, u - UPB + 1)
                cut = slice(it * P, (it + 1) * P)
                hh, hl, lh = (wi_hi, xT_hi), (wi_hi, xT_lo), (wi_lo, xT_hi)
                order = [(0, hh), (0, hl), (1, hh), (0, lh), (1, lh), (1, hl)]
                for n, (k, (w, xs)) in enumerate(order):
                    if it == 0:
                        pe.wait_ge(tx_lo if xs is xT_lo else tx_hi, KH * blk + k + 1)
                    if blk == 0 and k == 0 and xs is xT_hi:
                        pe.wait_ge(wi0_lo if w is wi_lo else wi0_hi, it * WC // NI + 1)
                    if blk == BPS and it == 0 and n == 0:
                        pe.wait_ge(wi1_lo, POOL_CHUNK)
                        pe.wait_ge(wi1_lo_p, WC - POOL_CHUNK)
                    last = nc.tensor.matmul(up[u % UPB][:], w[:, b, k, cut], xs[:, s, k, :],
                                            start=(n == 0), stop=(n == len(order) - 1))
                last.then_inc(up_done, 1)

            def down_tile(d):
                blk, t = divmod(d, TB)
                b = blk // BPS
                if d >= 2:
                    pe.wait_ge(r_done, d - 1)
                cut = slice(t * P, (t + 1) * P)
                new_wo = t == 0 and blk in (0, BPS)
                parts = [(h_hi, wo_hi), (h_lo, wo_hi), (h_hi, wo_lo)] if t == 0 and blk == 0 else \
                        [(h_hi, wo_hi), (h_hi, wo_lo), (h_lo, wo_hi)]
                if t == 0:
                    order = [(k, part) for part in parts[:2] for k in range(NI - 1)] \
                        + [(NI - 1, part) for part in parts[:2]] + [(k, parts[2]) for k in range(NI)]
                else:
                    order = [(k, part) for k in range(NI) for part in parts]
                for n, (k, (h, w)) in enumerate(order):
                    if t == 0:
                        pe.wait_ge(hlo_done if h is h_lo else gelu_done, blk * NI + k + 1)
                    if new_wo:
                        c = k // KCUT
                        if w is wo_hi and blk == 0:
                            pe.wait_ge(wo0_hi, c + 1)
                        elif w is wo_hi:
                            pe.wait_ge(w1_hi, WC + c + 1)
                        elif blk == BPS and c < POOL_CHUNK:
                            pe.wait_ge(wo1_lo, c + 1)
                        elif blk == BPS:
                            pe.wait_ge(wo1_lo_p, 1)
                        elif c < WC - WD:
                            pe.wait_ge(wo0_lo_p, c + 1)
                        else:
                            pe.wait_ge(wo0_lo_d, c + 1 - (WC - WD))
                    last = nc.tensor.matmul(dn[d % 2][:, 0:H], h[:, k, cut], w[:, b, k, :],
                                            start=(n == 0), stop=(n == len(order) - 1))
                    if blk >= 1 and (t, n) == (1, 12):
                        hs_transposes(blk - 1)
                    if blk == 3:
                        beside(t, n)
                last.then_inc(down_done, 1)

            def beside(t, n):
                if (t, n) == (1, 3):
                    pe.wait_ge(alg_dve, 1)
                    pe.wait_ge(setup_act, 3)
                    pe.wait_ge(gelu_done, NB * NI)
                    nc.tensor.matmul(up[2][R:2 * R, 0:R], gram[R:2 * R, :], LnT[R:2 * R, :],
                                     start=True, stop=True)
                    for j in range(KH):
                        small = nc.tensor.matmul(misc[:, j * R:(j + 1) * R], UT[:, j * P:(j + 1) * P],
                                                 LnT[0:R, :], start=True, stop=True)
                    small.then_inc(alg_pe, 1)
                if (t, n) == (1, 9):
                    pe.wait_ge(alg_dve, 3)
                    nc.tensor.matmul(up[2][0:R, 0:R], LnT[R:2 * R, :], gw_sb[R:2 * R, :],
                                     start=True, stop=True)
                    nc.tensor.matmul(misc[0:R, 0:H], uo_top[:], rwT[:], start=True, stop=True)\
                      .then_inc(alg_pe, 1)
                if (t, n) == (1, 15):
                    pe.wait_ge(alg_dve, 4)
                    nc.tensor.matmul(misc[0:96, 0:H], vtv[:].rearrange("p j r -> p (j r)"), ur[:],
                                     start=True, stop=True).then_inc(alg_pe, 1)
                if (t, n) == (1, 10):
                    project(0)
                if (t, n) == (2, 12):
                    response(0)
                    response(1)
                    project(1)
                if (t, n) == (3, 0):
                    hs_transposes(3)
                if (t, n) == (3, 8):
                    response(2)
                    response(3)
                if (t, n) == (3, 16):
                    project(2)

            def project(j):
                g = PROJ_ORDER[j]
                d, n = GROUPS[g]
                blk, t = divmod(d, TB)
                if j == 0:
                    pe.wait_ge(alg_dve, 3)
                if j >= 2:
                    pe.wait_ge(pj_lo, j - 1)
                pe.wait_ge(gelu_done, NB * NI)
                pe.wait_ge(th_out, KH * (g + 1) if g < len(GROUPS) - 1 else KH * g + 1)
                for k in range(KH):
                    last = nc.tensor.matmul(up[j % 2][0:96, 0:n * P],
                                            urep[:, k, :, :].rearrange("p j r -> p (j r)"),
                                            hsT[:, blk, k, t * P:(t + n) * P],
                                            start=(k == 0), stop=(k == KH - 1))
                last.then_inc(pj_done, 1)

            def last_sums(t):
                d, n = GROUPS[-1]
                pe.wait_ge(hs_done, d + t + 1)
                if t == 0:
                    pe.wait_ge(th_out, KH * (len(GROUPS) - 1))
                    pe.wait_ge(r_done, NT)
                for k in range(KH):
                    last = nc.tensor.matmul(sum_banks[k][:, 0:1], xr[:, d + t, k * P:(k + 1) * P],
                                            ones[:], start=(t == 0), stop=(t == n - 1))
                if t == n - 1:
                    last.then_inc(sum_pe, 1)

            def gate_hidden(b, last_group):
                groups = (range(BPS), range(BPS, len(GROUPS)))[b]
                if b == 0:
                    pe.wait_ge(th_out, KH * BPS)
                elif last_group:
                    pe.wait_ge(sum_dve, KH)
                else:
                    pe.wait_ge(th_out, KH * (len(GROUPS) - 1))
                    pe.wait_ge(fin_dve, 4)
                for g in groups[-1:] if last_group else groups[:-1]:
                    for k in range(KH):
                        last = nc.tensor.matmul(misc[0:GH, 4:5], w1T[:, k, :], hs_sum[:, g, k:k + 1],
                                                start=(g == groups[0] and k == 0),
                                                stop=(g == groups[-1] and k == KH - 1))
                if last_group:
                    last.then_inc(z_done, 1)

            def gate_out(b):
                pe.wait_ge(g_act, 2 * b + 1)
                nc.tensor.matmul(misc[:, 8:9], w2rep[:], h1[:, b:b + 1], start=True, stop=True)\
                  .then_inc(z_done, 1)

            def response(j):
                d = RESP_ORDER[j]
                group = [g for g, (first, n) in enumerate(GROUPS) if first <= d < first + n][0]
                pe.wait_ge(pj_lo, PROJ_ORDER.index(group) + 1)
                if j == 0:
                    pe.wait_ge(rhs_dve, 1)
                    pe.wait_ge(rows_act, 1)
                if 2 <= j < 5:
                    pe.wait_ge(fin_dve, j - 1)
                elif j == 5:
                    pe.wait_ge(r_done, NT - 1)
                elif j > 5:
                    pe.wait_ge(sum_dve, KH)
                for t in range(2):
                    last = nc.tensor.matmul(resp_banks[j][:, t * H:(t + 1) * H],
                                            proj[:, (d + t) * P:(d + t + 1) * P],
                                            resp_rhs[:], start=True, stop=True)
                last.then_inc(fin_pe, 1)

            pe.wait_ge(consts, 1)
            keep_warm(WARM)
            x_transposes(0, 0)
            pe.wait_ge(uv_in, 32)
            for m in range(2):
                for k in range(KH):
                    last = nc.tensor.matmul(dn[0][m * R:(m + 1) * R, 0:R], UV[:, m, k, :], UV[:, m, k, :],
                                            start=(k == 0), stop=(k == KH - 1))
            last.then_inc(gram_pe, 1)
            x_transposes(0, 1)
            pe.wait_ge(bi_in, 32)
            nc.tensor.transpose(misc[:, 0:B * NI], bi_sb[:], ident[0:B * NI, 0:B * NI])\
              .then_inc(setup_pe, 1)

            for blk in range(NB):
                for it in range(NI):
                    up_unit(blk * NI + it)
                if blk + 1 < NB:
                    for k in range(KH):
                        x_transposes(blk + 1, k)
                for t in range(TB):
                    if blk == 0 and t == 1:
                        pe.wait_ge(gate_in, 80)
                        pe.wait_ge(setup_act, 1)
                        for k in range(KH):
                            last = nc.tensor.transpose(misc[:, k * GH:(k + 1) * GH],
                                                       w1_sb[:, k * P:(k + 1) * P], ident[0:GH, 0:GH])
                        last.then_inc(setup_pe, 1)
                    if blk == 0 and t == 2:
                        pe.wait_ge(rw_in, 16)
                        pe.wait_ge(setup_act, 2)
                        for k in range(KH):
                            nc.tensor.transpose(misc[0:R, k * P:(k + 1) * P], UV[:, 0, k, :], ident[:])
                        for k in range(KH):
                            last = nc.tensor.transpose(misc[0:R, H + k * P:H + (k + 1) * P],
                                                       rw[:, k, :], ident[:])
                        last.then_inc(setup_pe, 1)
                    if blk == 2 and t == 2:
                        pe.wait_ge(gate_dve, 1)
                        gate_hidden(0, False)
                        gate_hidden(0, True)
                    if blk == 2 and t == 3:
                        gate_out(0)
                    down_tile(blk * TB + t)
            project(3)
            response(4)
            last_transposes(0)
            last_sums(0)
            gate_hidden(1, False)
            last_sums(1)
            last_transposes(1)
            gate_hidden(1, True)
            pe.wait_ge(pj_lo, 3)
            keep_warm(2)
            gate_out(1)
            response(5)
            response(6)
            project(4)
            response(7)


_INS = ["x", "itok_B_0_7", "condB_safetyscore", "L0_cond_Wi", "L0_cond_bi", "L0_cond_Wo", "L0_cond_bo",
        "L0_cond_gamma", "L0_cond_beta", "L1_cond_U", "L1_cond_V", "L1_cond_safety_bias",
        "L1_cond_gate_w1", "L1_cond_gate_b1", "L1_cond_gate_w2", "L1_cond_gate_b2", "L1_cond_resp_w",
        "L1_cond_resp_b"]


def kernel(**inputs):
    import numpy as _np
    import concourse.bacc as _bacc
    from concourse import mybir as _mybir
    from concourse.bass_utils import run_bass_kernel_spmd as _run

    nc = _bacc.Bacc("TRN2", target_bir_lowering=False, num_devices=1)
    arrays, args = {}, []
    for name in _INS:
        a = _np.ascontiguousarray(inputs[name])
        arrays[f"in_{name}"] = a
        args.append(nc.dram_tensor(f"in_{name}", a.shape, _mybir.dt.from_np(a.dtype), kind="ExternalInput").ap())
    out = nc.dram_tensor("out_0", (B, S, H), _mybir.dt.float32, kind="ExternalOutput").ap()
    cond_seq_kernel(nc, *args, out)
    r = _run(nc, [arrays], core_ids=[0])
    return r.results[0]["out_0"]
```
